# Optimizing a Trainium2 kernel written in Bass

```python
import numpy as np
import jax
import jax.numpy as jnp

def _softmax(x, axis=-1):
    return jax.nn.softmax(x, axis=axis)

def _gelu(x):
    return jax.nn.gelu(x, approximate=True)

def _silu(x):
    return jax.nn.silu(x)

def _sigmoid(x):
    return jax.nn.sigmoid(x)

def _layernorm(x, axis=-1, eps=1e-05):
    m = jnp.mean(x, axis=axis, keepdims=True)
    v = jnp.var(x, axis=axis, keepdims=True)
    return (x - m) / jnp.sqrt(v + eps)

def _scatter_add(tgt, idx, src, axis=0):
    return tgt.at[idx].add(src)

def _segment_sum(src, seg, n):
    return jax.ops.segment_sum(src, seg, n)
kernel_name = 'mk_conv_attn_hybrid_d2_conv_nchw256_r2_cb2fa0'

def setup_inputs(seed: int=0):
    np.random.seed(seed)
    _w = jnp.asarray

    def _rec_inputs():
        import jax
        import jax.numpy as jnp
        _gk = jax.random.key(seed)
        x = 7.22e-05 + 1 * jax.random.normal(jax.random.fold_in(_gk, 1), (8, 128, 32, 32), jnp.float32)
        return x
    x = _rec_inputs()

    def _L0_conv_setup():
        import jax, jax.numpy as jnp
        import numpy as np
        DIM = 128
        QK = 128
        HEADS = 8
        NWIN = 16
        TOPK = 4
        MLP_RATIO = 4
        SCALE = QK ** (-0.5)

        def _dwconv(x, w, b, pad):
            out = jax.lax.conv_general_dilated(x, w, (1, 1), [(pad, pad), (pad, pad)], feature_group_count=x.shape[1], dimension_numbers=('NCHW', 'OIHW', 'NCHW'))
            return out + b[None, :, None, None]

        def _bra(x, wq, gq, bq, wkv, gkv, bkv, w_lepe, b_lepe):
            N, C, H, W = x.shape
            j = i = NWIN
            h, w_ = (H // j, W // i)
            p2, w2 = (j * i, h * w_)
            xh = x.transpose(0, 2, 3, 1)
            xw = xh.reshape(N, j, h, i, w_, C).transpose(0, 1, 3, 2, 4, 5).reshape(N, p2, h, w_, C)
            q = xw @ wq.T * gq + bq
            kv = xw @ wkv.T * gkv + bkv
            q_pix = q.reshape(N, p2, w2, QK)
            kv_pix = kv.reshape(N, p2, w2, QK + C)
            q_win = q.mean((2, 3))
            k_win = kv[..., :QK].mean((2, 3))
            v_img = kv[..., QK:].reshape(N, j, i, h, w_, C).transpose(0, 1, 3, 2, 4, 5).reshape(N, H, W, C)
            lepe = _dwconv(v_img.transpose(0, 3, 1, 2), w_lepe, b_lepe, 2).transpose(0, 2, 3, 1)
            qd = jax.lax.stop_gradient(q_win)
            kd = jax.lax.stop_gradient(k_win)
            logit = qd * SCALE @ kd.transpose(0, 2, 1)
            _, r_idx = jax.lax.top_k(logit, TOPK)
            kv_sel = jax.vmap(lambda kvp, idx: kvp[idx])(kv_pix, r_idx)
            ch_k, ch_v = (QK // HEADS, C // HEADS)
            k_sel = kv_sel[..., :QK].reshape(N, p2, TOPK * w2, HEADS, ch_k).transpose(0, 1, 3, 2, 4)
            v_sel = kv_sel[..., QK:].reshape(N, p2, TOPK * w2, HEADS, ch_v).transpose(0, 1, 3, 2, 4)
            qh = q_pix.reshape(N, p2, w2, HEADS, ch_k).transpose(0, 1, 3, 2, 4)
            attn = jax.nn.softmax(jnp.einsum('npmqc,npmkc->npmqk', qh * SCALE, k_sel), axis=-1)
            out = jnp.einsum('npmqk,npmkc->npmqc', attn, v_sel)
            out = out.transpose(0, 1, 3, 2, 4).reshape(N, j, i, h, w_, C)
            out = out.transpose(0, 1, 3, 2, 4, 5).reshape(N, H, W, C)
            out = out + lepe
            return out.transpose(0, 3, 1, 2)
        key = jax.random.key(seed)
        ks = jax.random.split(key, 8)
        p = lambda k, shp: jax.random.normal(k, shp, jnp.float32) * 0.02
        hid = MLP_RATIO * DIM
        return {'x': jax.random.normal(ks[0], (8, DIM, 32, 32), jnp.float32), 'wq': p(ks[1], (QK, DIM)), 'gq': jnp.ones((QK,), jnp.float32), 'bq': jnp.zeros((QK,), jnp.float32), 'wkv': p(ks[2], (QK + DIM, DIM)), 'gkv': jnp.ones((QK + DIM,), jnp.float32), 'bkv': jnp.zeros((QK + DIM,), jnp.float32), 'w_lepe': p(ks[3], (DIM, 1, 5, 5)), 'b_lepe': jnp.zeros((DIM,), jnp.float32), 'w_fc1': p(ks[4], (hid, DIM)), 'g_fc1': jnp.ones((hid,), jnp.float32), 'b_fc1': jnp.zeros((hid,), jnp.float32), 'w_dw': p(ks[5], (hid, 1, 3, 3)), 'b_dw': jnp.zeros((hid,), jnp.float32), 'w_fc2': p(ks[6], (DIM, hid)), 'g_fc2': jnp.ones((DIM,), jnp.float32), 'b_fc2': jnp.zeros((DIM,), jnp.float32)}
    _L0_conv_all = _L0_conv_setup()
    _L0_conv_in = {k: v for k, v in _L0_conv_all.items() if k in ('wq', 'gq', 'bq', 'wkv', 'gkv', 'bkv', 'w_lepe', 'b_lepe', 'w_fc1', 'g_fc1', 'b_fc1', 'w_dw', 'b_dw', 'w_fc2', 'g_fc2', 'b_fc2')}
    del _L0_conv_all

    def _L1_attn_setup():
        import jax, jax.numpy as jnp
        import numpy as np
        N_HEADS = 4
        key = jax.random.key(seed)
        B, S, D = (4, 1024, 128)
        ks = jax.random.split(key, 9)
        sd = 1.0 / np.sqrt(D)
        return {'x': jax.random.normal(ks[0], (B, S, D), jnp.float32), 'Wq': jax.random.normal(ks[1], (D, D), jnp.float32) * sd, 'bq': jax.random.normal(ks[2], (D,), jnp.float32) * 0.02, 'Wk': jax.random.normal(ks[3], (D, D), jnp.float32) * sd, 'bk': jax.random.normal(ks[4], (D,), jnp.float32) * 0.02, 'Wv': jax.random.normal(ks[5], (D, D), jnp.float32) * sd, 'bv': jax.random.normal(ks[6], (D,), jnp.float32) * 0.02, 'Wo': jax.random.normal(ks[7], (D, D), jnp.float32) * sd, 'bo': jax.random.normal(ks[8], (D,), jnp.float32) * 0.02}
    _L1_attn_all = _L1_attn_setup()
    _L1_attn_in = {k: v for k, v in _L1_attn_all.items() if k in ('Wq', 'bq', 'Wk', 'bk', 'Wv', 'bv', 'Wo', 'bo')}
    del _L1_attn_all

    def _L1_ffn_setup():
        import jax, jax.numpy as jnp
        import numpy as np
        NUM_EXPERTS = 8
        TOP_K = 2
        B, S, D = (8, 4096, 128)

        def _moe(tokens, router_w, w1, b1, w2, b2):
            N = tokens.shape[0]
            E = router_w.shape[0]
            logits = tokens.astype(jnp.float32) @ router_w.astype(jnp.float32).T
            probs = jax.nn.softmax(logits, axis=-1)
            rw, re = jax.lax.top_k(probs, TOP_K)
            if TOP_K > 1:
                rw = rw / jnp.maximum(rw.sum(-1, keepdims=True), 1e-12)
            rw = rw.astype(tokens.dtype)
            combine = jnp.zeros((N, E), tokens.dtype).at[jnp.arange(N)[:, None], re].set(rw)
            out = tokens
            for e in range(E):
                h = jax.nn.gelu(tokens @ w1[e] + b1[e], approximate=False)
                y = h @ w2[e] + b2[e]
                out = out + combine[:, e:e + 1] * y
            return out
        key = jax.random.key(seed)
        ks = jax.random.split(key, 4)
        scale = 1.0 / np.sqrt(D).astype(np.float32)
        return {'input_embeddings': jax.random.normal(ks[0], (B, S, D), jnp.float32), 'router_w': jax.random.normal(ks[1], (NUM_EXPERTS, D), jnp.float32) * scale, 'w1': jax.random.normal(ks[2], (NUM_EXPERTS, D, D), jnp.float32) * scale, 'b1': jnp.zeros((NUM_EXPERTS, D), jnp.float32), 'w2': jax.random.normal(ks[3], (NUM_EXPERTS, D, D), jnp.float32) * scale, 'b2': jnp.zeros((NUM_EXPERTS, D), jnp.float32)}
    _L1_ffn_all = _L1_ffn_setup()
    _L1_ffn_in = {k: v for k, v in _L1_ffn_all.items() if k in ('router_w', 'w1', 'b1', 'w2', 'b2')}
    del _L1_ffn_all
    return {'x': x, 'L0_conv_wq': _L0_conv_in['wq'], 'L0_conv_gq': _L0_conv_in['gq'], 'L0_conv_bq': _L0_conv_in['bq'], 'L0_conv_wkv': _L0_conv_in['wkv'], 'L0_conv_gkv': _L0_conv_in['gkv'], 'L0_conv_bkv': _L0_conv_in['bkv'], 'L0_conv_w_lepe': _L0_conv_in['w_lepe'], 'L0_conv_b_lepe': _L0_conv_in['b_lepe'], 'L0_conv_w_fc1': _L0_conv_in['w_fc1'], 'L0_conv_g_fc1': _L0_conv_in['g_fc1'], 'L0_conv_b_fc1': _L0_conv_in['b_fc1'], 'L0_conv_w_dw': _L0_conv_in['w_dw'], 'L0_conv_b_dw': _L0_conv_in['b_dw'], 'L0_conv_w_fc2': _L0_conv_in['w_fc2'], 'L0_conv_g_fc2': _L0_conv_in['g_fc2'], 'L0_conv_b_fc2': _L0_conv_in['b_fc2'], 'L1_attn_Wq': _L1_attn_in['Wq'], 'L1_attn_bq': _L1_attn_in['bq'], 'L1_attn_Wk': _L1_attn_in['Wk'], 'L1_attn_bk': _L1_attn_in['bk'], 'L1_attn_Wv': _L1_attn_in['Wv'], 'L1_attn_bv': _L1_attn_in['bv'], 'L1_attn_Wo': _L1_attn_in['Wo'], 'L1_attn_bo': _L1_attn_in['bo'], 'L1_ffn_router_w': _L1_ffn_in['router_w'], 'L1_ffn_w1': _L1_ffn_in['w1'], 'L1_ffn_b1': _L1_ffn_in['b1'], 'L1_ffn_w2': _L1_ffn_in['w2'], 'L1_ffn_b2': _L1_ffn_in['b2']}

def reference(x, L0_conv_wq, L0_conv_gq, L0_conv_bq, L0_conv_wkv, L0_conv_gkv, L0_conv_bkv, L0_conv_w_lepe, L0_conv_b_lepe, L0_conv_w_fc1, L0_conv_g_fc1, L0_conv_b_fc1, L0_conv_w_dw, L0_conv_b_dw, L0_conv_w_fc2, L0_conv_g_fc2, L0_conv_b_fc2, L1_attn_Wq, L1_attn_bq, L1_attn_Wk, L1_attn_bk, L1_attn_Wv, L1_attn_bv, L1_attn_Wo, L1_attn_bo, L1_ffn_router_w, L1_ffn_w1, L1_ffn_b1, L1_ffn_w2, L1_ffn_b2):
    import jax
    import jax.numpy as jnp

    def _L0_conv_ref(x, wq, gq, bq, wkv, gkv, bkv, w_lepe, b_lepe, w_fc1, g_fc1, b_fc1, w_dw, b_dw, w_fc2, g_fc2, b_fc2):
        import jax, jax.numpy as jnp
        import numpy as np
        DIM = 128
        QK = 128
        HEADS = 8
        NWIN = 16
        TOPK = 4
        MLP_RATIO = 4
        SCALE = QK ** (-0.5)

        def _dwconv(x, w, b, pad):
            out = jax.lax.conv_general_dilated(x, w, (1, 1), [(pad, pad), (pad, pad)], feature_group_count=x.shape[1], dimension_numbers=('NCHW', 'OIHW', 'NCHW'))
            return out + b[None, :, None, None]

        def _bra(x, wq, gq, bq, wkv, gkv, bkv, w_lepe, b_lepe):
            N, C, H, W = x.shape
            j = i = NWIN
            h, w_ = (H // j, W // i)
            p2, w2 = (j * i, h * w_)
            xh = x.transpose(0, 2, 3, 1)
            xw = xh.reshape(N, j, h, i, w_, C).transpose(0, 1, 3, 2, 4, 5).reshape(N, p2, h, w_, C)
            q = xw @ wq.T * gq + bq
            kv = xw @ wkv.T * gkv + bkv
            q_pix = q.reshape(N, p2, w2, QK)
            kv_pix = kv.reshape(N, p2, w2, QK + C)
            q_win = q.mean((2, 3))
            k_win = kv[..., :QK].mean((2, 3))
            v_img = kv[..., QK:].reshape(N, j, i, h, w_, C).transpose(0, 1, 3, 2, 4, 5).reshape(N, H, W, C)
            lepe = _dwconv(v_img.transpose(0, 3, 1, 2), w_lepe, b_lepe, 2).transpose(0, 2, 3, 1)
            qd = jax.lax.stop_gradient(q_win)
            kd = jax.lax.stop_gradient(k_win)
            logit = qd * SCALE @ kd.transpose(0, 2, 1)
            _, r_idx = jax.lax.top_k(logit, TOPK)
            kv_sel = jax.vmap(lambda kvp, idx: kvp[idx])(kv_pix, r_idx)
            ch_k, ch_v = (QK // HEADS, C // HEADS)
            k_sel = kv_sel[..., :QK].reshape(N, p2, TOPK * w2, HEADS, ch_k).transpose(0, 1, 3, 2, 4)
            v_sel = kv_sel[..., QK:].reshape(N, p2, TOPK * w2, HEADS, ch_v).transpose(0, 1, 3, 2, 4)
            qh = q_pix.reshape(N, p2, w2, HEADS, ch_k).transpose(0, 1, 3, 2, 4)
            attn = jax.nn.softmax(jnp.einsum('npmqc,npmkc->npmqk', qh * SCALE, k_sel), axis=-1)
            out = jnp.einsum('npmqk,npmkc->npmqc', attn, v_sel)
            out = out.transpose(0, 1, 3, 2, 4).reshape(N, j, i, h, w_, C)
            out = out.transpose(0, 1, 3, 2, 4, 5).reshape(N, H, W, C)
            out = out + lepe
            return out.transpose(0, 3, 1, 2)
        x = x + _bra(x, wq, gq, bq, wkv, gkv, bkv, w_lepe, b_lepe)
        h1 = jnp.einsum('nchw,dc->ndhw', x, w_fc1) * g_fc1[None, :, None, None] + b_fc1[None, :, None, None]
        h1 = jax.nn.relu(_dwconv(h1, w_dw, b_dw, 1))
        h2 = jnp.einsum('nchw,dc->ndhw', h1, w_fc2) * g_fc2[None, :, None, None] + b_fc2[None, :, None, None]
        return x + h2

    def _L1_attn_ref(x, Wq, bq, Wk, bk, Wv, bv, Wo, bo):
        import jax, jax.numpy as jnp
        import numpy as np
        N_HEADS = 4
        B, S, D = x.shape
        H = N_HEADS
        W = D // H

        def heads(t):
            return t.reshape(B, S, H, W).transpose(0, 2, 1, 3)
        q = heads(x @ Wq + bq)
        k = heads(x @ Wk + bk)
        v = heads(x @ Wv + bv)
        scores = jnp.einsum('bhqw,bhkw->bhqk', q, k) / jnp.sqrt(jnp.float32(W))
        i = jnp.arange(S, dtype=jnp.float32)
        mask = (S - jnp.abs(i[:, None] - i[None, :])) / S
        scores = jax.nn.softmax(scores * mask, axis=-1)
        h = jnp.einsum('bhqk,bhkw->bhqw', scores, v)
        h = h.transpose(0, 2, 1, 3).reshape(B, S, D)
        return h @ Wo + bo

    def _L1_ffn_ref(input_embeddings, router_w, w1, b1, w2, b2):
        import jax, jax.numpy as jnp
        import numpy as np
        NUM_EXPERTS = 8
        TOP_K = 2
        B, S, D = (8, 4096, 128)

        def _moe(tokens, router_w, w1, b1, w2, b2):
            N = tokens.shape[0]
            E = router_w.shape[0]
            logits = tokens.astype(jnp.float32) @ router_w.astype(jnp.float32).T
            probs = jax.nn.softmax(logits, axis=-1)
            rw, re = jax.lax.top_k(probs, TOP_K)
            if TOP_K > 1:
                rw = rw / jnp.maximum(rw.sum(-1, keepdims=True), 1e-12)
            rw = rw.astype(tokens.dtype)
            combine = jnp.zeros((N, E), tokens.dtype).at[jnp.arange(N)[:, None], re].set(rw)
            out = tokens
            for e in range(E):
                h = jax.nn.gelu(tokens @ w1[e] + b1[e], approximate=False)
                y = h @ w2[e] + b2[e]
                out = out + combine[:, e:e + 1] * y
            return out
        b, s, d = input_embeddings.shape
        tokens = input_embeddings.reshape(b * s, d)
        return _moe(tokens, router_w, w1, b1, w2, b2).reshape(b, s, d)

    def _gn(v, G=32, eps=1e-05):
        B_, C_, H_, W_ = v.shape
        g = v.reshape(B_, G, C_ // G, H_, W_)
        m = jnp.mean(g, axis=(2, 3, 4), keepdims=True)
        s = jnp.var(g, axis=(2, 3, 4), keepdims=True)
        return ((g - m) / jnp.sqrt(s + eps)).reshape(v.shape)

    def _ln_c(v, eps=1e-06):
        m = jnp.mean(v, axis=1, keepdims=True)
        s = jnp.var(v, axis=1, keepdims=True)
        return (v - m) / jnp.sqrt(s + eps)

    def _ln_t(v, eps=1e-05):
        m = jnp.mean(v, axis=-1, keepdims=True)
        s = jnp.var(v, axis=-1, keepdims=True)
        return (v - m) / jnp.sqrt(s + eps)

    def _to_tokens(v):
        B_, C_, H_, W_ = v.shape
        return v.reshape(B_, C_, H_ * W_).transpose(0, 2, 1)

    def _from_tokens(t, like):
        B_, C_, H_, W_ = like.shape
        return t.transpose(0, 2, 1).reshape(B_, C_, H_, W_)
    x = _L0_conv_ref(x, L0_conv_wq, L0_conv_gq, L0_conv_bq, L0_conv_wkv, L0_conv_gkv, L0_conv_bkv, L0_conv_w_lepe, L0_conv_b_lepe, L0_conv_w_fc1, L0_conv_g_fc1, L0_conv_b_fc1, L0_conv_w_dw, L0_conv_b_dw, L0_conv_w_fc2, L0_conv_g_fc2, L0_conv_b_fc2)
    t = _to_tokens(x)
    t = t + _L1_attn_ref(_ln_t(t), L1_attn_Wq, L1_attn_bq, L1_attn_Wk, L1_attn_bk, L1_attn_Wv, L1_attn_bv, L1_attn_Wo, L1_attn_bo)
    t = t + _L1_ffn_ref(_ln_t(t), L1_ffn_router_w, L1_ffn_w1, L1_ffn_b1, L1_ffn_w2, L1_ffn_b2)
    x = _from_tokens(t, x)
    return x

_drawn_inputs = setup_inputs


def setup_inputs(seed=0):
    import zlib

    import numpy as np

    out = dict(_drawn_inputs(seed))
    spreads = {'L0_conv_gq': (1.0, 0.2),
     'L0_conv_bq': (0.0, 0.1),
     'L0_conv_gkv': (1.0, 0.2),
     'L0_conv_bkv': (0.0, 0.1),
     'L0_conv_b_lepe': (0.0, 0.1),
     'L0_conv_g_fc1': (1.0, 0.6),
     'L0_conv_b_fc1': (0.0, 0.739),
     'L0_conv_b_dw': (0.0, 0.1),
     'L0_conv_g_fc2': (1.0, 0.6),
     'L0_conv_b_fc2': (0.0, 0.1),
     'L1_ffn_b1': (0.0, 0.323),
     'L1_ffn_b2': (0.0, 0.1)}
    factors = {'L0_conv_w_fc1': 5.1, 'L0_conv_w_dw': 4.712, 'L1_attn_bq': 24.251, 'L1_attn_bk': 172.119}
    for name, (base, spread) in spreads.items():
        noise = np.random.default_rng([zlib.crc32(name.encode()), seed]).standard_normal(out[name].shape)
        drawn = base * np.exp(spread * noise) if base else spread * noise
        out[name] = jnp.asarray(drawn.astype(out[name].dtype))
    for name, factor in factors.items():
        out[name] = (out[name] * factor).astype(out[name].dtype)
    return out
```

```python
from contextlib import ExitStack

import concourse.bass as bass
from concourse import mybir

F32 = mybir.dt.float32
U32 = mybir.dt.uint32
ALU = mybir.AluOpType
ACT = mybir.ActivationFunctionType
AX = mybir.AxisListType

IMAGES, C, SIDE = 8, 128, 32
TOK = SIDE * SIDE
HALF = TOK // 2
WIN_SIDE = SIDE // 2
WINS = WIN_SIDE * WIN_SIDE
WTILES = WINS // 128
PX = 4
SLOTS = 4
KEYS = SLOTS * PX
HEADS_A, CH_A = 8, 16
SCALE_A = float(C) ** -0.5
LSIDE = SIDE + 4
TAPS5 = 25
GROUPS = 4
MSIDE = SIDE + 2
TAPS3 = 9
HEADS_C, CH_C = 4, 32
TT = TOK // 128
QCHUNK = 256
QCHUNKS = TOK // QCHUNK
UNITS = QCHUNKS * HEADS_C * (QCHUNK // 128)
PER_CHUNK = UNITS // QCHUNKS
LN_EPS = 1e-5
EXPERTS = 8
BAND = 2 * TOK - 128

SECTIONS = [("wqkv", 384), ("qkv_bias", 384), ("fc1", 512), ("fc2", 512), ("attn_w", 512), ("bv_row", 128),
            ("router", EXPERTS), ("w1", 1024), ("w2", 1024), ("b2", 128), ("lepe_w", TAPS5),
            ("dw_w", GROUPS * TAPS3), ("bq_a", 1), ("bk_a", 1), ("bv_a", 1), ("b_lepe", 1),
            ("g_fc1", GROUPS), ("b_fc1", GROUPS), ("b_dw", GROUPS), ("b_fc2", 1),
            ("bq_c", 1), ("bk_c", 1), ("bo_c", 1), ("b1", EXPERTS),
            ("ident", 128), ("mean_w", 128), ("band", BAND), ("iota", TT * EXPERTS), ("eps", 1)]
COLUMN = {}
_at = 0
for _name, _width in SECTIONS:
    COLUMN[_name] = (_at, _width)
    _at += _width
PACKED = _at


class Ring:

    def __init__(self, entries, slots):
        self.place, self.uses = {}, [0] * slots
        for i, name in enumerate(entries):
            s = i % slots
            self.place[name] = (s, self.uses[s])
            self.uses[s] += 1

    def slot(self, name):
        return self.place[name][0]

    def turn(self, name, n):
        s, k = self.place[name]
        return n * self.uses[s] + k + 1


RING_A = Ring([("qkv", t, h) for t in range(WTILES) for h in range(2)] + ["v", "windows", "logits", "attended"], 1)


def main_order():
    order = [("fc1", 0), ("fc1", 1), ("dw", 0), ("fc1", 2), ("dw", 1), ("fc1", 3), ("dw", 2), ("dw", 3), "fc2"]
    order += [("mean", 0), ("var", 0), ("rstd", 0), "q", "k", "v", ("scores", 0), ("scores", 1)]
    for u in range(UNITS):
        order.append(("turned", u))
        if u + 2 < UNITS:
            order.append(("scores", u + 2))
        if u % PER_CHUNK == PER_CHUNK - 1:
            order.append(("pv", u // PER_CHUNK))
    order += ["wo", ("mean", 1), ("var", 1), ("rstd", 1), "router", ("hidden", 0), ("hidden", 1), "combine", "start"]
    for e in range(EXPERTS):
        order.append(("expert", e))
        if e + 2 < EXPERTS:
            order.append(("hidden", e + 2))
    return order


ORDER_B = main_order()
RING_B = Ring(ORDER_B, 3)

LINKS_A = 44
LINKS_B = 75


def hybrid_layers(nc, x, x_by_window, packed, gains, out, table):
    with ExitStack() as ctx:
        def sb(name, shape, dt=F32):
            return ctx.enter_context(nc.sbuf_tensor(name, shape, dt))

        def sem(name):
            return ctx.enter_context(nc.semaphore(name))

        W = sb("W", [128, PACKED])

        def w(name, a=0, b=None):
            at, width = COLUMN[name]
            return W[:, at + a:at + (width if b is None else b)]

        def col(name, i=0):
            return w(name, i, i + 1)

        X = sb("X", [128, TOK])
        Q = sb("Q", [128, WTILES, PX, C])
        KV = sb("KV", [128, WTILES, PX, 2 * C])
        V_PAD = sb("V_PAD", [128, LSIDE, LSIDE])
        QWIN = sb("QWIN", [128, WINS])
        KWIN = sb("KWIN", [128, WINS])
        KVSEL = sb("KVSEL", [128, WTILES, KEYS, 2 * C])
        PROD = sb("PROD", [128, KEYS * C])
        S = sb("S", [128, PX, KEYS, HEADS_A])
        SUMS = sb("SUMS", [128, 2, PX * HEADS_A])
        TOP = sb("TOP", [128, WTILES, 8])
        CHOSEN = sb("CHOSEN", [128, WTILES, 8], U32)
        XLEPE = sb("XLEPE", [128, TOK])
        X_SUM4 = PROD[:, 0:WINS]
        TAP = KV[:, 0].rearrange("p x c -> p (x c)")
        XR = sb("XR", [128, TOK])
        DIAG = sb("DIAG", [128, GROUPS * TAPS3, 128])
        H1_PAD = sb("H1_PAD", [128, 2, MSIDE, MSIDE])
        PT = sb("PT", [128, HEADS_C, TT, QCHUNK])
        H2 = PT[:, 0:2].rearrange("p h t q -> p (h t q)").rearrange("p (g n) -> p g n", g=GROUPS)
        TN = sb("TN", [128, TOK])
        SQ = sb("SQ", [128, TOK])
        ATT = SQ
        QZ = sb("QZ", [128, HEADS_C, TOK])
        KT = sb("KT", [128, TOK])
        V = sb("V", [128, TT, C])
        P = sb("P", [128, 2, TOK])
        HG = P
        NEGMAX = sb("NEGMAX", [128, 2, 2])
        L = sb("L", [128, 2, QCHUNK // 128, HEADS_C])
        RX = sb("RX", [128, QCHUNK // 128, HEADS_C, CH_C])
        RT = sb("RT", [128, QCHUNK])
        STD = sb("STD", [128, TT])
        ACC = sb("ACC", [128, TT, C])
        PROBS = sb("PROBS", [128, TT, EXPERTS])
        RSTAT = sb("RSTAT", [128, 4, TT])
        BEST = sb("BEST", [128, TT, 8])
        BEST_AT = sb("BEST_AT", [128, TT, 8], U32)
        BEST_ATF = sb("BEST_ATF", [128, TT, 2])
        BEST_W = sb("BEST_W", [128, TT, 2])
        PICK = sb("PICK", [128, 2, TT, EXPERTS])
        COMB = sb("COMB", [128, TT, EXPERTS])
        COMB_T = KT[0:EXPERTS, :]

        psA = ctx.enter_context(nc.psum_tensor("psA", [128, 2 * HALF], F32))
        psB = [ctx.enter_context(nc.psum_tensor(f"psB{i}", [128, 2 * HALF], F32)) for i in range(3)]

        weights_in = sem("weights_in")
        ready = sem("ready")
        x_in, raster_in, out_done = sem("x_in"), sem("raster_in"), sem("out_done")
        a_ready, a_free = sem("a_ready"), sem("a_free")
        b_ready = [sem(f"b_ready{i}") for i in range(3)]
        b_free = [sem(f"b_free{i}") for i in range(3)]
        xsum_ready, kv_ready, table_in = sem("xsum_ready"), sem("kv_ready"), sem("table_in")
        v_ready, tap_ready, win_ready, chosen_ready = sem("v_ready"), sem("tap_ready"), sem("win_ready"), sem("chosen_ready")
        kvsel_in = [sem(f"kvsel_in{t}") for t in range(WTILES)]
        s_ready, e_ready, attended_ready = sem("s_ready"), sem("e_ready"), sem("attended_ready")
        pv_done, lepe_done, x1_ready = sem("pv_done"), sem("lepe_done"), sem("x1_ready")
        h1_ready, h2_ready, x2_ready = sem("h1_ready"), sem("h2_ready"), sem("x2_ready")
        centred_ready, square_ready, std_ready, norm_ready = (
            sem("centred_ready"), sem("square_ready"), sem("std_ready"), sem("norm_ready"))
        rstd_ready = sem("rstd_ready")
        qk_ready, vt_ready = sem("qk_ready"), sem("vt_ready")
        scaled_ready, p_ready, pt_ready = sem("scaled_ready"), sem("p_ready"), sem("pt_ready")
        rx_ready, att_ready = sem("rx_ready"), sem("att_ready")
        sum_ready, rsub_ready, rexp_ready = sem("sum_ready"), sem("rsub_ready"), sem("rexp_ready")
        comb_ready, combt_ready = sem("comb_ready"), sem("combt_ready")
        acc_ready, hg_ready, out_ready = sem("acc_ready"), sem("hg_ready"), sem("out_ready")
        fences = {e: sem(f"fence_{e}") for e in ("DVE", "Pool", "SP")}
        dve_a, dve_b = sem("dve_a"), sem("dve_b")

        table_rows = table.rearrange("(t p) f -> p t f", p=128)
        ident = w("ident")

        def fence(engine):
            engine.sem_inc(fences[engine.engine.name], 1)

        block = ctx.enter_context(nc.Block())

        @block.sync
        def _(sp):
            def load_x(m):
                sp.dma_start(X[:], x_by_window[bass.ds(m, 1)].rearrange("a c n -> (a c) n")).then_inc(x_in, 16)

            def load_raster(m):
                if not (isinstance(m, int) and m == 0):
                    sp.wait_ge(x1_ready, m)
                sp.dma_start(XLEPE[:], x[bass.ds(m, 1)].rearrange("a c n -> (a c) n")).then_inc(raster_in, 16)

            def x_is_free(m):
                sp.wait_ge(a_ready, RING_A.turn("v", m - 1))
                sp.wait_ge(xsum_ready, m)

            def store_table(m):
                sp.wait_ge(kv_ready, 2 * WTILES * (m + 1))
                fence(sp)
                for t in range(WTILES):
                    if not (isinstance(m, int) and m == 0):
                        sp.wait_ge(kvsel_in[t], 16 * SLOTS * m)
                sp.dma_start(table_rows, KV[:].rearrange("p t x c -> p t (x c)")).then_inc(table_in, 16)

            def store_out(n):
                sp.wait_ge(out_ready, n + 1)
                sp.dma_start(out[bass.ds(n, 1)].rearrange("a (t p) c -> p (a t) c", p=128), ACC[:]).then_inc(out_done, 16)

            sp.dma_start(W[:], packed).then_inc(weights_in, 16)
            sp.dma_start(PROD[:, 0:512], gains).then_inc(weights_in, 16)
            load_x(0)
            load_raster(0)
            store_table(0)
            x_is_free(1)
            load_x(1)
            with sp.Fori(0, IMAGES - 2) as n:
                load_raster(n + 1)
                store_table(n + 1)
                x_is_free(n + 2)
                load_x(n + 2)
                store_out(n)
                fence(sp)
            load_raster(IMAGES - 1)
            store_table(IMAGES - 1)
            store_out(IMAGES - 2)
            store_out(IMAGES - 1)
            sp.wait_ge(out_done, 16 * (IMAGES + 1))

        @block.tensor
        def _(pe):
            def two_halves(ps, lhs, rhs, **kw):
                for h in range(2):
                    mm = pe.matmul(ps[:, h * HALF:(h + 1) * HALF], lhs, rhs[:, h * HALF:(h + 1) * HALF], **kw)
                return mm

            whole = dict(start=True, stop=True)

            def open_a(name, m):
                pe.wait_ge(a_free, RING_A.turn(name, m))

            def a_projections(m):
                pe.wait_ge(x_in, 16 * (m + 1))
                for t in range(WTILES):
                    for hy in range(2):
                        open_a(("qkv", t, hy), m)
                        for wx in range(2):
                            at = (2 * hy + wx) * WINS + t * 128
                            px = X[:, at:at + 128]
                            mm = pe.matmul(psA[:, wx * HALF:wx * HALF + 384], px, w("wqkv"), **whole)
                        mm.then_inc(a_ready, 1)
                open_a("v", m)
                two_halves(psA, w("wqkv", 256, 384), X, **whole).then_inc(a_ready, 1)
                pe.wait_ge(xsum_ready, m + 1)
                open_a("windows", m)
                pe.matmul(psA[:, 0:WINS], w("wqkv", 0, 128), X_SUM4, **whole)
                pe.matmul(psA[:, HALF:HALF + WINS], w("wqkv", 128, 256), X_SUM4, **whole).then_inc(a_ready, 1)

            def a_logits(m):
                pe.wait_ge(win_ready, 2 * (m + 1))
                open_a("logits", m)
                for t in range(WTILES):
                    mm = pe.matmul(psA[:, t * HALF:t * HALF + WINS], QWIN[:, t * 128:(t + 1) * 128], KWIN[:], **whole)
                mm.then_inc(a_ready, 1)

            def a_attended(m):
                pe.wait_ge(attended_ready, WTILES * (m + 1))
                open_a("attended", m)
                for t in range(WTILES):
                    for p in range(PX):
                        at = t * HALF + p * 128
                        mm = pe.transpose(psA[:, at:at + 128], Q[:, t, p, :], ident)
                mm.then_inc(a_ready, 1)

            def emit(name, n):
                s = RING_B.slot(name)
                ps = psB[s]
                kind, i = name if isinstance(name, tuple) else (name, 0)
                if kind == "fc1" and i == 0:
                    pe.wait_ge(x1_ready, n + 1)
                if kind == "dw":
                    pe.wait_ge(h1_ready, GROUPS * n + i + 1)
                if kind == "fc2":
                    pe.wait_ge(h2_ready, GROUPS * (n + 1))
                if kind == "mean":
                    pe.wait_ge(x2_ready, 2 * n + i + 1)
                if kind == "var":
                    pe.wait_ge(square_ready, 2 * n + i + 1)
                if kind == "rstd":
                    pe.wait_ge(rstd_ready, 2 * n + i + 1)
                if kind in ("q", "router"):
                    pe.wait_ge(norm_ready, 2 * n + (kind == "router") + 1)
                if kind == "scores" and i == 0:
                    pe.wait_ge(qk_ready, 2 * (n + 1))
                if kind == "turned":
                    pe.wait_ge(p_ready, UNITS * n + i + 1)
                if kind == "pv":
                    pe.wait_ge(vt_ready, n + 1)
                    pe.wait_ge(pt_ready, UNITS * n + PER_CHUNK * (i + 1))
                    pe.wait_ge(rx_ready, QCHUNKS * n + i + 1)
                if kind == "wo":
                    pe.wait_ge(att_ready, QCHUNKS * (n + 1))
                if kind == "combine":
                    pe.wait_ge(comb_ready, n + 1)
                if kind == "start":
                    pe.wait_ge(combt_ready, n + 1)
                    pe.wait_ge(sum_ready, n + 1)
                if kind == "expert":
                    pe.wait_ge(hg_ready, EXPERTS * n + i + 1)
                pe.wait_ge(b_free[s], RING_B.turn(name, n))
                if kind == "fc1":
                    mm = two_halves(ps, w("fc1", 128 * i, 128 * i + 128), XR, **whole)
                elif kind == "dw":
                    for tap in range(TAPS3):
                        dy, dx = divmod(tap, 3)
                        for h in range(2):
                            rows = H1_PAD[:, i % 2, 16 * h + dy:16 * h + dy + 16, dx:dx + SIDE]
                            mm = pe.matmul(ps[:, h * HALF:(h + 1) * HALF], DIAG[:, TAPS3 * i + tap, :], rows,
                                           start=tap == 0, stop=tap == TAPS3 - 1)
                elif kind == "fc2":
                    for g in range(GROUPS):
                        mm = two_halves(ps, w("fc2", 128 * g, 128 * g + 128), H2[:, g, :],
                                        start=g == 0, stop=g == GROUPS - 1)
                elif kind == "mean":
                    mm = two_halves(ps, w("mean_w"), XR, **whole)
                elif kind == "var":
                    for t in range(TT):
                        mm = pe.matmul(ps[:, t:t + 1], SQ[:, t * 128:(t + 1) * 128], w("mean_w", 0, 1), **whole)
                elif kind == "rstd":
                    for t in range(TT):
                        mm = pe.transpose(ps[:, t * 128:(t + 1) * 128], SQ[:, t * 128:(t + 1) * 128], ident)
                elif kind in ("q", "k", "wo"):
                    at = {"q": 0, "k": 128, "wo": 384}[kind]
                    mm = two_halves(ps, w("attn_w", at, at + 128), ATT if kind == "wo" else TN, **whole)
                elif kind == "v":
                    for t in range(TT):
                        mm = pe.matmul(ps[:, t * 128:(t + 1) * 128], TN[:, t * 128:(t + 1) * 128],
                                       w("attn_w", 256, 384), **whole)
                elif kind == "scores":
                    h, q = unit(i)
                    mm = two_halves(ps, QZ[:, h, q * 128:(q + 1) * 128], KT, **whole)
                elif kind == "turned":
                    for t in range(TT):
                        mm = pe.transpose(ps[:, t * 128:(t + 1) * 128], P[:, i % 2, t * 128:(t + 1) * 128], ident)
                elif kind == "pv":
                    for j in range(QCHUNK // 128):
                        pe.transpose(ps[:, HALF + j * 128:HALF + (j + 1) * 128],
                                     RX[:, j].rearrange("p h c -> p (h c)"), ident)
                    for t in range(TT):
                        for h in range(HEADS_C):
                            rows = slice(CH_C * h, CH_C * (h + 1))
                            mm = pe.matmul(ps[rows, 0:QCHUNK], V[:, t, rows], PT[:, h, t, :],
                                           start=t == 0, stop=t == TT - 1)
                elif kind == "router":
                    for t in range(TT):
                        mm = pe.matmul(ps[:, t * EXPERTS:(t + 1) * EXPERTS], TN[:, t * 128:(t + 1) * 128],
                                       w("router"), **whole)
                elif kind == "combine":
                    for t in range(TT):
                        mm = pe.transpose(ps[0:EXPERTS, t * 128:(t + 1) * 128], COMB[:, t, :], ident)
                elif kind == "start":
                    for t in range(TT):
                        cols = slice(t * 128, (t + 1) * 128)
                        pe.matmul(ps[:, cols], XR[:, cols], ident, start=True, stop=False)
                        mm = pe.matmul(ps[:, cols], COMB_T[:, cols], w("b2")[0:EXPERTS], start=False, stop=True)
                elif kind == "hidden":
                    mm = two_halves(ps, w("w1", 128 * i, 128 * i + 128), TN, **whole)
                elif kind == "expert":
                    for t in range(TT):
                        mm = pe.matmul(ps[:, t * 128:(t + 1) * 128], HG[:, i % 2, t * 128:(t + 1) * 128],
                                       w("w2", 128 * i, 128 * i + 128), **whole)
                mm.then_inc(b_ready[s], 1)

            def stages_b_to_d(n, m):
                if m is not None:
                    a_projections(m)
                for name in ORDER_B:
                    emit(name, n)
                    if m is not None and name == ("fc1", 1):
                        a_logits(m)
                    if m is not None and name == ("expert", 0):
                        a_attended(m)

            pe.wait_ge(weights_in, 32)
            pe.wait_ge(ready, 3)
            a_projections(0)
            a_logits(0)
            a_attended(0)
            with pe.Fori(0, IMAGES - 1) as n:
                stages_b_to_d(n, n + 1)
            stages_b_to_d(IMAGES - 1, None)

        @block.scalar
        def _(act):
            def a_evacuate(m):
                act.wait_ge(a_ready, RING_A.turn("v", m))
                if not (isinstance(m, int) and m == 0):
                    act.wait_ge(lepe_done, TAPS5 * m)
                for p in range(PX):
                    hy, wx = divmod(p, 2)
                    act.activation(V_PAD[:, 2 + hy:2 + hy + SIDE:2, 2 + wx:2 + wx + SIDE:2],
                                   psA[:, p * WINS:(p + 1) * WINS].rearrange("c (j i) -> c j i", i=WIN_SIDE),
                                   ACT.Identity, bias=col("bv_a")).then_inc(v_ready, 1)
                act.wait_ge(v_ready, PX * (m + 1))
                act.sem_inc(a_free, 1)
                act.wait_ge(a_ready, RING_A.turn("windows", m))
                act.activation(QWIN[:], psA[:, 0:WINS], ACT.Identity, bias=col("bq_a"),
                               scale=1.0 / PX).then_inc(win_ready, 1)
                act.activation(KWIN[:], psA[:, HALF:HALF + WINS], ACT.Identity, bias=col("bk_a"),
                               scale=1.0 / PX).then_inc(win_ready, 1)
                act.wait_ge(win_ready, 2 * (m + 1))
                act.sem_inc(a_free, 1)

            def a_exp(t, m):
                act.wait_ge(s_ready, WTILES * m + t + 1)
                act.activation(S[:], S[:], ACT.Exp, scale=SCALE_A).then_inc(e_ready, 1)

            def evacuate(name, n, signal, *ops):
                s = RING_B.slot(name)
                act.wait_ge(b_ready[s], RING_B.turn(name, n))
                for op in ops[:-1]:
                    op(psB[s])
                ops[-1](psB[s]).then_inc(b_free[s], 1)
                act.wait_ge(b_free[s], RING_B.turn(name, n) + 1)
                act.sem_inc(signal, 1)

            def fc1(g, n):
                evacuate(("fc1", g), n, h1_ready, lambda ps: act.activation(
                    H1_PAD[:, g % 2, 1:1 + SIDE, 1:1 + SIDE], ps[:].rearrange("c (y x) -> c y x", y=SIDE),
                    ACT.Identity, bias=col("b_fc1", g), scale=col("g_fc1", g)))

            def dw(g, n):
                evacuate(("dw", g), n, h2_ready, lambda ps: act.activation(
                    H2[:, g, :], ps[:], ACT.Relu, bias=col("b_dw", g)))

            def norm(i, n):
                act.wait_ge(centred_ready, 2 * n + i + 1)
                act.activation(SQ[:], TN[:], ACT.Square).then_inc(square_ready, 1)
                evacuate(("var", i), n, std_ready, lambda ps: act.activation(
                    STD[:], ps[:, 0:TT], ACT.Sqrt, bias=col("eps")))

            def exp(u, n):
                act.wait_ge(scaled_ready, UNITS * n + u + 1)
                h, q = unit(u)
                act.activation(P[:, u % 2, :], P[:, u % 2, :], ACT.Exp, bias=NEGMAX[:, u % 2, 1:2],
                               accum_out=L[:, u // PER_CHUNK % 2, q % 2, h:h + 1]).then_inc(p_ready, 1)

            def turned(u, n):
                h, q = unit(u)
                evacuate(("turned", u), n, pt_ready, lambda ps: act.activation(
                    PT[:, h, :, (q % 2) * 128:(q % 2) * 128 + 128], ps[:].rearrange("k (t q) -> k t q", t=TT), ACT.Copy))

            def stages_b_to_d(n, m):
                if m is not None:
                    a_evacuate(m)
                fc1(0, n)
                fc1(1, n)
                dw(0, n)
                fc1(2, n)
                dw(1, n)
                fc1(3, n)
                dw(2, n)
                if m is not None:
                    a_exp(0, m)
                dw(3, n)
                norm(0, n)
                evacuate("q", n, qk_ready, *[
                    lambda ps, h=h: act.activation(QZ[CH_C * h:CH_C * (h + 1), h, :], ps[CH_C * h:CH_C * (h + 1), :],
                                                   ACT.Identity, bias=col("bq_c")[CH_C * h:CH_C * (h + 1)])
                    for h in range(HEADS_C)])
                evacuate("k", n, qk_ready, lambda ps: act.activation(KT[:], ps[:], ACT.Identity, bias=col("bk_c")))
                exp(0, n)
                for u in range(UNITS):
                    if u + 1 < UNITS:
                        exp(u + 1, n)
                    turned(u, n)
                    if m is not None and u == 6:
                        a_exp(1, m)
                norm(1, n)
                act.wait_ge(rsub_ready, n + 1)
                act.activation(PROBS[:], PROBS[:], ACT.Exp).then_inc(rexp_ready, 1)

                def gelu(e):
                    evacuate(("hidden", e), n, hg_ready, lambda ps: act.activation(
                        HG[:, e % 2, :], ps[:], ACT.Gelu, bias=col("b1", e)))

                gelu(0)
                gelu(1)
                evacuate("combine", n, combt_ready, lambda ps: act.activation(COMB_T[:], ps[0:EXPERTS, :], ACT.Copy))
                act.wait_ge(out_done, 16 * (n + 1))
                evacuate("start", n, acc_ready, lambda ps: act.activation(
                    ACC[:].rearrange("p t c -> p (t c)"), ps[:], ACT.Copy))
                for e in range(2, EXPERTS):
                    gelu(e)

            act.wait_ge(weights_in, 32)
            act.wait_ge(ready, 3)
            a_evacuate(0)
            a_exp(0, 0)
            a_exp(1, 0)
            with act.Fori(0, IMAGES - 1) as n:
                stages_b_to_d(n, n + 1)
            stages_b_to_d(IMAGES - 1, None)

        @block.vector
        def _(dve):
            class Chain:

                def __init__(self, signal, per_image):
                    self.sem, self.per_image, self.k = signal, per_image, 0

                def at_image(self, n):
                    self.base, self.k = n * self.per_image, 0

                def link(self, ins):
                    self.k += 1
                    ins.then_inc(self.sem, 1)
                    dve.wait_ge(self.sem, self.base + self.k)

                def fill(self):
                    assert self.k == self.per_image, (self.sem, self.k)

            chain_a, chain_b = Chain(dve_a, LINKS_A), Chain(dve_b, LINKS_B)

            def a_steps(m):
                link = chain_a.link

                def sums():
                    chain_a.at_image(m)
                    dve.wait_ge(x_in, 16 * (m + 1))
                    dve.tensor_reduce(X_SUM4, X[:].rearrange("c (p w) -> c w p", p=PX), AX.X,
                                      ALU.add).then_inc(xsum_ready, 1)

                def rows(t, hy):
                    dve.wait_ge(a_ready, RING_A.turn(("qkv", t, hy), m))
                    if t == 0 and hy == 0 and not (isinstance(m, int) and m == 0):
                        dve.wait_ge(table_in, 16 * m)
                    ps = psA[:].rearrange("p (x c) -> p x c", x=2)
                    bias = w("qkv_bias").unsqueeze(1)
                    dve.tensor_tensor(Q[:, t, 2 * hy:2 * hy + 2, :], ps[:, :, 0:128],
                                      bias[:, :, 0:128].broadcast_to([128, 2, 128]), ALU.add)
                    link(dve.tensor_tensor(KV[:, t, 2 * hy:2 * hy + 2, :], ps[:, :, 128:384],
                                           bias[:, :, 128:384].broadcast_to([128, 2, 256]), ALU.add))
                    dve.sem_inc(kv_ready, 1)
                    dve.sem_inc(a_free, 1)

                def choose():
                    dve.wait_ge(a_ready, RING_A.turn("logits", m))
                    for t in range(WTILES):
                        logits = psA[:, t * HALF:t * HALF + WINS]
                        fence(dve)
                        link(dve.max(TOP[:, t, :], logits))
                        fence(dve)
                        last = dve.max_index(CHOSEN[:, t, :], TOP[:, t, :], logits)
                    link(last)
                    dve.sem_inc(a_free, 1)
                    dve.sem_inc(chosen_ready, 1)

                def scores(t, q):
                    if q == 0:
                        dve.wait_ge(kvsel_in[t], 16 * SLOTS * (m + 1))
                    link(dve.tensor_tensor(PROD[:].rearrange("p (k c) -> p k c", k=KEYS), KVSEL[:, t, :, 0:C],
                                           Q[:, t, q, :].unsqueeze(1).broadcast_to([128, KEYS, C]), ALU.mult))
                    link(dve.tensor_reduce(S[:, q].rearrange("p k h -> p (k h)"),
                                           PROD[:].rearrange("p (k c) -> p k c", c=CH_A), AX.X, ALU.add))

                def softmax_head(t):
                    top, by_head = SUMS[:, 0, :], S[:].rearrange("p q k h -> p q h k")
                    link(dve.tensor_reduce(top.rearrange("p (q h) -> p q h", q=PX), by_head, AX.X, ALU.max))
                    dve.tensor_tensor(S[:], S[:], top.rearrange("p (q h) -> p q h", q=PX).unsqueeze(2)
                                      .broadcast_to([128, PX, KEYS, HEADS_A]), ALU.subtract).then_inc(s_ready, 1)

                def softmax_tail(t):
                    dve.wait_ge(e_ready, WTILES * m + t + 1)
                    link(dve.tensor_reduce(SUMS[:, 0, :].rearrange("p (q h) -> p q h", q=PX),
                                           S[:].rearrange("p q k h -> p q h k"), AX.X, ALU.add))
                    dve.reciprocal(SUMS[:, 1, :], SUMS[:, 0, :])

                def attend(t, q):
                    probs = S[:, q].rearrange("p k h -> p (k h)").unsqueeze(2).broadcast_to([128, KEYS * HEADS_A, CH_A])
                    link(dve.tensor_tensor(PROD[:].rearrange("p (k h c) -> p k h c", k=KEYS, h=HEADS_A),
                                           KVSEL[:, t, :, C:2 * C].rearrange("p k (h c) -> p k h c", h=HEADS_A),
                                           S[:, q].unsqueeze(3).broadcast_to([128, KEYS, HEADS_A, CH_A]), ALU.mult))
                    link(dve.tensor_reduce(Q[:, t, q, :], PROD[:].rearrange("p (k f) -> p f k", k=KEYS), AX.X, ALU.add))
                    if q == PX - 1:
                        dve.sem_inc(pv_done, 1)
                        heads = Q[:, t].rearrange("p q (h c) -> p (q h) c", h=HEADS_A)
                        dve.tensor_tensor(heads, heads, SUMS[:, 1, :].unsqueeze(2)
                                          .broadcast_to([128, PX * HEADS_A, CH_A]), ALU.mult).then_inc(attended_ready, 1)

                def residual():
                    dve.wait_ge(lepe_done, TAPS5 * (m + 1))
                    dve.wait_ge(a_ready, RING_A.turn("attended", m))
                    if not (isinstance(m, int) and m == 0):
                        s = RING_B.slot("start")
                        dve.wait_ge(b_ready[s], RING_B.turn("start", m - 1))
                    for t in range(WTILES):
                        for hy in range(2):
                            raster = "c (j hy i wx) -> c hy j i wx"
                            dims = dict(j=WIN_SIDE, hy=2, i=WIN_SIDE, wx=2)
                            rows_of = slice(8 * t, 8 * t + 8)
                            ps = psA[:, t * HALF + hy * 256:t * HALF + hy * 256 + 256].rearrange(
                                "c (wx j i) -> c j i wx", wx=2, j=8)
                            for wx in range(2):
                                last = dve.scalar_tensor_tensor(
                                    out=XR[:].rearrange(raster, **dims)[:, hy, rows_of, :, wx],
                                    in0=ps[:, :, :, wx], scalar=col("b_lepe"),
                                    in1=XLEPE[:].rearrange(raster, **dims)[:, hy, rows_of, :, wx],
                                    op0=ALU.add, op1=ALU.add)
                    link(last)
                    dve.sem_inc(a_free, 1)
                    dve.sem_inc(x1_ready, 1)
                    chain_a.fill()

                steps = [sums] + [lambda t=t, hy=hy: rows(t, hy) for t in range(WTILES) for hy in range(2)] + [choose]
                for t in range(WTILES):
                    steps += [lambda t=t, q=q: scores(t, q) for q in range(PX)]
                    steps += [lambda t=t: softmax_head(t), lambda t=t: softmax_tail(t)]
                    steps += [lambda t=t, q=q: attend(t, q) for q in range(PX)]
                return steps + [residual]

            def stages_b_to_d(n, m):
                link = chain_b.link
                chain_b.at_image(n)
                steps = a_steps(m) if m is not None else []

                def run_a(count):
                    for _ in range(min(count, len(steps))):
                        steps.pop(0)()

                def arrived(name):
                    s = RING_B.slot(name)
                    dve.wait_ge(b_ready[s], RING_B.turn(name, n))
                    return psB[s], b_free[s]

                def residual_add(name, bias):
                    ps, free = arrived(name)
                    link(dve.scalar_tensor_tensor(out=XR[:], in0=ps[:], scalar=bias, in1=XR[:],
                                                  op0=ALU.add, op1=ALU.add))
                    dve.sem_inc(free, 1)
                    dve.sem_inc(x2_ready, 1)

                def centre(i):
                    ps, free = arrived(("mean", i))
                    link(dve.tensor_tensor(TN[:], XR[:], ps[:], ALU.subtract))
                    dve.sem_inc(free, 1)
                    dve.sem_inc(centred_ready, 1)

                def normalise(i):
                    dve.wait_ge(std_ready, 2 * n + i + 1)
                    link(dve.reciprocal(STD[:], STD[:]))
                    dve.tensor_copy(SQ[:].rearrange("p (t c) -> p t c", t=TT), STD[:].unsqueeze(2)
                                    .broadcast_to([128, TT, C])).then_inc(rstd_ready, 1)
                    ps, free = arrived(("rstd", i))
                    link(dve.tensor_tensor(TN[:], TN[:], ps[:], ALU.mult))
                    dve.sem_inc(free, 1)
                    dve.sem_inc(norm_ready, 1)

                def scale_scores(u):
                    ps, free = arrived(("scores", u))
                    if u >= 2:
                        before = ("turned", u - 2)
                        dve.wait_ge(b_ready[RING_B.slot(before)], RING_B.turn(before, n))
                    q = unit(u)[1]
                    at = TOK - 128 - 128 * q
                    fence(dve)
                    link(dve.tensor_tensor_reduce(P[:, u % 2, :], ps[:], w("band", at, at + TOK), 1.0, -3.0e38,
                                                  ALU.mult, ALU.max, NEGMAX[:, u % 2, 0:1]))
                    dve.sem_inc(free, 1)
                    dve.tensor_scalar(NEGMAX[:, u % 2, 1:2], NEGMAX[:, u % 2, 0:1], -1.0, None,
                                      ALU.mult).then_inc(scaled_ready, 1)

                def normaliser(c):
                    dve.wait_ge(p_ready, UNITS * n + PER_CHUNK * (c + 1))
                    if c > 0:
                        before = ("pv", c - 1)
                        dve.wait_ge(b_ready[RING_B.slot(before)], RING_B.turn(before, n))
                    sums = L[:, c % 2]
                    link(dve.reciprocal(sums, sums))
                    dve.tensor_copy(RX[:], sums.unsqueeze(3).broadcast_to([128, QCHUNK // 128, HEADS_C, CH_C])
                                    ).then_inc(rx_ready, 1)

                def attended(c):
                    ps, free = arrived(("pv", c))
                    link(dve.tensor_copy(RT[:], ps[:, HALF:HALF + QCHUNK]))
                    link(dve.tensor_tensor(ATT[:, QCHUNK * c:QCHUNK * (c + 1)], ps[:, 0:QCHUNK], RT[:], ALU.mult))
                    dve.sem_inc(free, 1)
                    dve.sem_inc(att_ready, 1)

                run_a(5)
                run_a(1)
                run_a(4)
                run_a(2)
                run_a(4)
                run_a(2)
                residual_add("fc2", col("b_fc2"))
                centre(0)
                normalise(0)
                run_a(1)
                ps, free = arrived("v")
                link(dve.tensor_tensor(V[:], ps[:].rearrange("p (t c) -> p t c", t=TT),
                                       w("bv_row").unsqueeze(1).broadcast_to([128, TT, C]), ALU.add))
                dve.sem_inc(free, 1)
                dve.sem_inc(vt_ready, 1)
                scale_scores(0)
                for u in range(UNITS):
                    if u + 1 < UNITS:
                        scale_scores(u + 1)
                    if u % 3 == 1 and len(steps) > 1:
                        run_a(1)
                    if u % PER_CHUNK == PER_CHUNK - 1:
                        normaliser(u // PER_CHUNK)
                        attended(u // PER_CHUNK)
                residual_add("wo", col("bo_c"))
                centre(1)
                normalise(1)
                dve.tensor_tensor(XR[:], XR[:], TN[:], ALU.add).then_inc(sum_ready, 1)
                ps, free = arrived("router")
                logits = ps[:, 0:TT * EXPERTS].rearrange("p (t e) -> p t e", t=TT)
                over_e = [128, TT, EXPERTS]
                link(dve.tensor_reduce(RSTAT[:, 0, :], logits, AX.X, ALU.max))
                link(dve.tensor_tensor(PROBS[:], logits, RSTAT[:, 0, :].unsqueeze(2).broadcast_to(over_e), ALU.subtract))
                dve.sem_inc(free, 1)
                dve.sem_inc(rsub_ready, 1)
                dve.wait_ge(rexp_ready, n + 1)
                link(dve.tensor_reduce(RSTAT[:, 1, :], PROBS[:], AX.X, ALU.add))
                link(dve.reciprocal(RSTAT[:, 2, :], RSTAT[:, 1, :]))
                link(dve.tensor_tensor(PROBS[:], PROBS[:], RSTAT[:, 2, :].unsqueeze(2).broadcast_to(over_e), ALU.mult))
                fence(dve)
                for t in range(TT):
                    last = dve.max(BEST[:, t, :], PROBS[:, t, :])
                link(last)
                fence(dve)
                for t in range(TT):
                    last = dve.max_index(BEST_AT[:, t, :], BEST[:, t, :], PROBS[:, t, :])
                link(last)
                link(dve.tensor_tensor(RSTAT[:, 0, :], BEST[:, :, 0], BEST[:, :, 1], ALU.add))
                link(dve.tensor_scalar(RSTAT[:, 1, :], RSTAT[:, 0, :], 1e-12, None, ALU.max))
                link(dve.reciprocal(RSTAT[:, 2, :], RSTAT[:, 1, :]))
                dve.tensor_tensor(BEST_W[:], BEST[:, :, 0:2], RSTAT[:, 2, :].unsqueeze(2).broadcast_to([128, TT, 2]), ALU.mult)
                link(dve.tensor_copy(BEST_ATF[:], BEST_AT[:, :, 0:2]))
                iota = w("iota").rearrange("p (t e) -> p t e", t=TT)
                for k in range(2):
                    last = dve.tensor_tensor(PICK[:, k], iota, BEST_ATF[:, :, k:k + 1].broadcast_to(over_e), ALU.is_equal)
                link(last)
                for k in range(2):
                    last = dve.tensor_tensor(PICK[:, k], PICK[:, k], BEST_W[:, :, k:k + 1].broadcast_to(over_e), ALU.mult)
                link(last)
                link(dve.tensor_tensor(COMB[:], PICK[:, 0], PICK[:, 1], ALU.add))
                dve.sem_inc(comb_ready, 1)
                dve.wait_ge(acc_ready, n + 1)
                for e in range(EXPERTS):
                    ps, free = arrived(("expert", e))
                    for t in range(TT):
                        last = dve.scalar_tensor_tensor(out=ACC[:, t, :], in0=ps[:, t * 128:(t + 1) * 128],
                                                        scalar=COMB[:, t, e:e + 1], in1=ACC[:, t, :],
                                                        op0=ALU.mult, op1=ALU.add)
                    link(last)
                    dve.sem_inc(free, 1)
                    if e == 1:
                        run_a(len(steps))
                dve.sem_inc(out_ready, 1)
                chain_b.fill()

            dve.wait_ge(weights_in, 32)
            dve.tensor_tensor(w("wqkv"), w("wqkv"), PROD[:, 0:384], ALU.mult)
            for g in range(GROUPS):
                wg = w("fc2", 128 * g, 128 * g + 128)
                last = dve.tensor_tensor(wg, wg, PROD[:, 384:512], ALU.mult)
            for i in range(GROUPS * TAPS3):
                last = dve.tensor_scalar(DIAG[:, i, :], ident, col("dw_w", i), None, ALU.mult)
            last.then_inc(ready, 1)
            dve.wait_ge(ready, 3)
            for step in a_steps(0):
                step()
            with dve.Fori(0, IMAGES - 1) as n:
                stages_b_to_d(n, n + 1)
            stages_b_to_d(IMAGES - 1, None)

        @block.gpsimd
        def _(pool):
            def gathers(m):
                pool.wait_ge(chosen_ready, m + 1)
                pool.wait_ge(table_in, 16 * (m + 1))
                if not (isinstance(m, int) and m == 0):
                    pool.wait_ge(pv_done, WTILES * m)
                fence(pool)
                for t in range(WTILES):
                    for s in range(SLOTS):
                        pool.indirect_dma_start(
                            KVSEL[:, t, PX * s:PX * (s + 1), :].rearrange("p x c -> p (x c)"), None, table,
                            bass.IndirectOffsetOnAxis(ap=CHOSEN[:, t, s:s + 1], axis=0)).then_inc(kvsel_in[t], 16)

            def taps(m):
                pool.wait_ge(raster_in, 16 * (m + 1))
                pool.wait_ge(v_ready, PX * (m + 1))
                acc = XLEPE[:].rearrange("c (y x) -> c y x", y=SIDE)
                product = TAP.rearrange("c (y x) -> c y x", y=SIDE)
                for tap in range(TAPS5):
                    dy, dx = divmod(tap, 5)
                    fence(pool)
                    pool.tensor_scalar(product, V_PAD[:, dy:dy + SIDE, dx:dx + SIDE], col("lepe_w", tap), 0.0,
                                       ALU.mult, ALU.add).then_inc(tap_ready, 1)
                    pool.wait_ge(tap_ready, TAPS5 * m + tap + 1)
                    pool.tensor_tensor(acc, acc, product, ALU.add).then_inc(lepe_done, 1)
                    pool.wait_ge(lepe_done, TAPS5 * m + tap + 1)

            pool.memset(V_PAD[:], 0.0).then_inc(ready, 1)
            pool.memset(H1_PAD[:], 0.0)
            pool.memset(QZ[:], 0.0).then_inc(ready, 1)
            pool.sem_inc(a_free, 1)
            for s in range(3):
                pool.sem_inc(b_free[s], 1)
            pool.sem_inc(out_done, 16)
            pool.wait_ge(weights_in, 32)
            gathers(0)
            taps(0)
            with pool.Fori(0, IMAGES - 1) as n:
                gathers(n + 1)
                taps(n + 1)


def unit(u):
    c, r = divmod(u, PER_CHUNK)
    return r // 2, 2 * c + r % 2


def kernel(**inputs):
    import numpy as np
    import concourse.bacc as bacc
    from concourse.bass_utils import run_bass_kernel_spmd

    a = {k: np.asarray(v) for k, v in inputs.items()}
    f32 = np.float32

    def cols(v):
        return v.reshape(-1, 128).T

    def everywhere(v):
        return np.broadcast_to(v.reshape(1, -1), (128, v.size))

    L0 = {k[8:]: v for k, v in a.items() if k.startswith("L0_conv_")}
    L1 = {k[3:]: v for k, v in a.items() if k.startswith("L1_")}
    b2 = np.zeros((128, 128), f32)
    b2[:EXPERTS] = L1["ffn_b2"]
    distance = np.abs(np.arange(BAND)[None, :] - (TOK - 128) - np.arange(128)[:, None])
    band = ((TOK - distance) / TOK / np.sqrt(CH_C)).astype(f32)
    parts = {
        "wqkv": np.concatenate([L0["wq"].T, L0["wkv"].T], 1),
        "qkv_bias": everywhere(np.concatenate([L0["bq"], L0["bkv"]])),
        "fc1": L0["w_fc1"].T,
        "fc2": L0["w_fc2"].T.reshape(GROUPS, 128, 128).transpose(1, 0, 2).reshape(128, -1),
        "attn_w": np.concatenate([L1["attn_Wq"], L1["attn_Wk"], L1["attn_Wv"], L1["attn_Wo"]], 1),
        "bv_row": everywhere(L1["attn_bv"]),
        "router": L1["ffn_router_w"].T,
        "w1": L1["ffn_w1"].transpose(1, 0, 2).reshape(128, -1),
        "w2": L1["ffn_w2"].transpose(1, 0, 2).reshape(128, -1),
        "b2": b2,
        "lepe_w": L0["w_lepe"].reshape(128, TAPS5),
        "dw_w": L0["w_dw"].reshape(GROUPS, 128, TAPS3).transpose(1, 0, 2).reshape(128, -1),
        "bq_a": cols(L0["bq"]), "bk_a": cols(L0["bkv"][:128]), "bv_a": cols(L0["bkv"][128:]),
        "b_lepe": cols(L0["b_lepe"]), "g_fc1": cols(L0["g_fc1"]), "b_fc1": cols(L0["b_fc1"]),
        "b_dw": cols(L0["b_dw"]), "b_fc2": cols(L0["b_fc2"]),
        "bq_c": cols(L1["attn_bq"]), "bk_c": cols(L1["attn_bk"]), "bo_c": cols(L1["attn_bo"]),
        "b1": L1["ffn_b1"].T,
        "ident": np.eye(128, dtype=f32),
        "mean_w": np.full((128, 128), 1.0 / 128, f32),
        "band": band,
        "iota": np.broadcast_to(np.tile(np.arange(EXPERTS, dtype=f32), TT), (128, TT * EXPERTS)),
        "eps": np.full((128, 1), LN_EPS, f32),
    }
    for name, width in SECTIONS:
        assert parts[name].shape == (128, width), (name, parts[name].shape)
    arrays = {
        "x_dram": np.ascontiguousarray(a["x"].reshape(IMAGES, C, TOK)),
        "x_by_window_dram": np.ascontiguousarray(a["x"].reshape(IMAGES, C, WIN_SIDE, 2, WIN_SIDE, 2)
                                                 .transpose(0, 1, 3, 5, 2, 4)).reshape(IMAGES, C, TOK),
        "packed_dram": np.ascontiguousarray(np.concatenate([parts[name] for name, _ in SECTIONS], 1)),
        "gains_dram": np.ascontiguousarray(everywhere(np.concatenate([L0["gq"], L0["gkv"], L0["g_fc2"]]))),
    }
    nc = bacc.Bacc("TRN2", target_bir_lowering=False, num_devices=1)
    args = [nc.dram_tensor(k, v.shape, F32, kind="ExternalInput").ap() for k, v in arrays.items()]
    out = nc.dram_tensor("out_dram", (IMAGES, TOK, C), F32, kind="ExternalOutput").ap()
    table = nc.dram_tensor("window_table", (WINS, PX * 2 * C), F32).ap()
    hybrid_layers(nc, *args, out, table)
    r = run_bass_kernel_spmd(nc, [arrays], core_ids=[0])
    got = r.results[0]["out_dram"]
    return np.ascontiguousarray(got.transpose(0, 2, 1)).reshape(IMAGES, C, SIDE, SIDE)
```

```python
from contextlib import ExitStack

import concourse.bass as bass
from concourse import mybir

F32 = mybir.dt.float32
F32R = mybir.dt.float32r
U32 = mybir.dt.uint32
ALU = mybir.AluOpType
ACT = mybir.ActivationFunctionType
AX = mybir.AxisListType

IMAGES, C, SIDE = 8, 128, 32
TOK = SIDE * SIDE
HALF = TOK // 2
WIN_SIDE = SIDE // 2
WINS = WIN_SIDE * WIN_SIDE
WTILES = WINS // 128
PX = 4
SLOTS = 4
KEYS = SLOTS * PX
HEADS_A, CH_A = 8, 16
SCALE_A = float(C) ** -0.5
LSIDE = SIDE + 4
TAPS5 = 25
GROUPS = 4
MSIDE = SIDE + 2
QUADS = GROUPS * 4
PLANE = MSIDE * MSIDE
DIAGONALS = QUADS * 3
HEADS_C, CH_C = 4, 32
TT = TOK // 128
UNITS = TT * HEADS_C
AHEAD = 3
P_BUFFERS = AHEAD
TURNED_BUFFERS = 2 * HEADS_C
LN_EPS = 1e-5
EXPERTS = 8
BAND = 2 * TOK - 128

SECTIONS = [("wqkv", 384), ("qkv_bias", 384), ("fc1", 512), ("fc2", 512), ("attn_q", 384), ("attn_k", 384),
            ("attn_vo", 256), ("bv_row", 128),
            ("router", EXPERTS), ("w1", 1024), ("w2", 1024), ("b2", 128), ("lepe_w", TAPS5),
            ("bq_a", 1), ("bk_a", 1), ("bv_a", 1), ("b_lepe", 1),
            ("g_fc1", GROUPS), ("b_fc1", GROUPS), ("b_dw", GROUPS), ("b_fc2", 1),
            ("bq_c", HEADS_C), ("bk_c", HEADS_C), ("bo_c", 1), ("b1", EXPERTS),
            ("ident", 128), ("mean_w", 128), ("band", BAND), ("iota", TT * EXPERTS), ("eps", 1)]
COLUMN = {}
_at = 0
for _name, _width in SECTIONS:
    COLUMN[_name] = (_at, _width)
    _at += _width
PACKED = _at


class Ring:

    def __init__(self, entries, slots):
        self.place, self.uses = {}, [0] * slots
        for i, name in enumerate(entries):
            s = i % slots
            self.place[name] = (s, self.uses[s])
            self.uses[s] += 1

    def slot(self, name):
        return self.place[name][0]

    def turn(self, name, n):
        s, k = self.place[name]
        return n * self.uses[s] + k + 1


class SharedRing(Ring):

    def __init__(self, first, middle, second, slots):
        super().__init__(first + middle + second, slots)
        self.first, self.middle = first, middle

    def turn(self, name, m):
        s, k = self.place[name]
        if name in self.middle:
            m = m + 1
        turn = m * self.uses[s] + k + 1
        if not (isinstance(m, int) and m == 0 and name in self.first):
            turn = turn - sum(self.place[other][0] == s for other in self.middle)
        if isinstance(m, int) and m == IMAGES:
            turn -= sum(self.place[other][0] == s for other in self.first)
        return turn


RING_A = SharedRing([("qkv", t, p) for t in range(WTILES) for p in range(PX)] + [("v", 0), ("v", 1), "windows", "logits"],
                    [("pv", t) for t in range(TT)], [("attended", t) for t in range(WTILES)], 2)


def main_order():
    order = [("fc1", 0), ("fc1", 1), ("dw", 0), ("fc1", 2), ("dw", 1), ("fc1", 3), ("dw", 2), ("dw", 3), "fc2"]
    order += [("mean", 0), ("var", 0), ("rstd", 0)] + ["v"]
    for h in range(HEADS_C):
        order += [("q", h), ("k", h)]
        if 0 < h:
            order.append(("scores", h - 1))
    for u in range(UNITS):
        order.append(("turned", u))
        if u + AHEAD < UNITS:
            order.append(("scores", u + AHEAD))
    order += ["wo", ("mean", 1), ("var", 1), ("rstd", 1), "router", ("hidden", 0), ("hidden", 1), "combine", "start"]
    for e in range(EXPERTS):
        order.append(("expert", e))
        if e + 2 < EXPERTS:
            order.append(("hidden", e + 2))
    return order


ORDER_B = main_order()
RING_B = Ring(ORDER_B, 3)

LINKS_A1 = 20
LINKS_A2 = 46
LINKS_B = 63


def hybrid_layers(nc, x, x_by_window, packed, gains, out, table):
    with ExitStack() as ctx:
        def sb(name, shape, dt=F32):
            return ctx.enter_context(nc.sbuf_tensor(name, shape, dt))

        def sem(name):
            return ctx.enter_context(nc.semaphore(name))

        W = sb("W", [128, PACKED])

        def w(name, a=0, b=None):
            at, width = COLUMN[name]
            return W[:, at + a:at + (width if b is None else b)]

        def col(name, i=0):
            return w(name, i, i + 1)

        X = sb("X", [128, TOK])
        Q = sb("Q", [128, WTILES, PX, C])
        KV = sb("KV", [128, WTILES, PX, 2 * C])
        V_PAD = sb("V_PAD", [128, LSIDE, LSIDE])
        KVSEL = sb("KVSEL", [128, WTILES, KEYS, 2 * C])
        PROD = sb("PROD", [128, KEYS * C])
        S = sb("S", [128, PX, KEYS, HEADS_A])
        SUMS = sb("SUMS", [128, 2, PX * HEADS_A])
        TOP = sb("TOP", [128, WTILES, 8])
        CHOSEN = sb("CHOSEN", [128, WTILES, 8], U32)
        XLEPE = sb("XLEPE", [128, TOK])
        X_SUM4, QWIN, KWIN = (PROD[:, i * WINS:(i + 1) * WINS] for i in range(3))
        TAP = KV[:, 0].rearrange("p x c -> p (x c)")
        XR = sb("XR", [128, TOK])
        DIAG = sb("DIAG", [128, DIAGONALS, 32])
        STACKED = sb("STACKED", [128, 2 * 4 * PLANE])
        SHIFTED = STACKED[:].rearrange("p (b q n) -> p b q n", b=2, q=4)
        QS = STACKED[:, 0:HEADS_C * TOK].rearrange("p (h n) -> p h n", h=HEADS_C)
        KS = STACKED[:, HEADS_C * TOK:2 * HEADS_C * TOK].rearrange("p (h n) -> p h n", h=HEADS_C)
        H1_PAD = sb("H1_PAD", [128, 2, MSIDE, MSIDE])
        PT = sb("PT", [128, TURNED_BUFFERS, TT, 128])
        H2 = PT[:, 0:GROUPS].rearrange("p g t q -> p g (t q)")
        TN = sb("TN", [128, TOK])
        SQ = sb("SQ", [128, TOK])
        ATT = SQ
        V = sb("V", [128, TT, C])
        P = sb("P", [128, P_BUFFERS, TOK])
        HG = P
        NEGMAX = sb("NEGMAX", [128, P_BUFFERS, 2])
        L = sb("L", [128, TT, HEADS_C])
        RX = TN[:, 0:2 * C].rearrange("p (b h c) -> p b h c", b=2, h=HEADS_C)
        RT = TN[:, 2 * C:3 * C]
        STD = sb("STD", [128, TT])
        ACC = PT[:, GROUPS]
        spare = PT[:, GROUPS + 1].rearrange("p t q -> p (t q)")
        PROBS, BEST, BEST_AT, COMB, PICK = (
            spare[:, i * TT * EXPERTS:(i + k) * TT * EXPERTS] for i, k in ((0, 1), (1, 1), (2, 1), (3, 1), (4, 2)))
        PROBS, BEST, BEST_AT, COMB = (v.rearrange("p (t e) -> p t e", t=TT) for v in (PROBS, BEST, BEST_AT, COMB))
        BEST_AT = BEST_AT.bitcast(U32)
        PICK = PICK.rearrange("p (k t e) -> p k t e", k=2, t=TT)
        RSTAT = spare[:, 6 * TT * EXPERTS:6 * TT * EXPERTS + 4 * TT].rearrange("p (i t) -> p i t", i=4)
        BEST_ATF, BEST_W = (spare[:, at:at + 2 * TT].rearrange("p (t k) -> p t k", t=TT)
                            for at in (7 * TT * EXPERTS, 8 * TT * EXPERTS))
        COMB_T = PT[0:EXPERTS, GROUPS - 1].rearrange("p t q -> p (t q)")

        psA = [ctx.enter_context(nc.psum_tensor(f"psA{i}", [128, HALF], F32)) for i in range(2)]
        psB = [ctx.enter_context(nc.psum_tensor(f"psB{i}", [128, 2 * HALF], F32)) for i in range(3)]

        weights_in = sem("weights_in")
        ready = sem("ready")
        x_in, raster_in, out_done = sem("x_in"), sem("raster_in"), sem("out_done")
        a_ready = [sem(f"a_ready{i}") for i in range(2)]
        a_free = [sem(f"a_free{i}") for i in range(2)]
        b_ready = [sem(f"b_ready{i}") for i in range(3)]
        b_free = [sem(f"b_free{i}") for i in range(3)]
        xsum_ready, kv_ready, table_in = sem("xsum_ready"), sem("kv_ready"), sem("table_in")
        v_ready, tap_ready, win_ready, chosen_ready = sem("v_ready"), sem("tap_ready"), sem("win_ready"), sem("chosen_ready")
        kvsel_in = [sem(f"kvsel_in{t}") for t in range(WTILES)]
        s_ready, e_ready, attended_ready = sem("s_ready"), sem("e_ready"), sem("attended_ready")
        pv_done, lepe_done, x1_ready = sem("pv_done"), sem("lepe_done"), sem("x1_ready")
        h1_ready, h2_ready, x2_ready = sem("h1_ready"), sem("h2_ready"), sem("x2_ready")
        shifted_in = [sem(f"shifted_in{b}") for b in range(2)]
        centred_ready, square_ready, std_ready, norm_ready = (
            sem("centred_ready"), sem("square_ready"), sem("std_ready"), sem("norm_ready"))
        rstd_ready = sem("rstd_ready")
        high_ready, qk_ready, vt_ready = sem("high_ready"), sem("qk_ready"), sem("vt_ready")
        scaled_ready, p_ready, pt_ready = sem("scaled_ready"), sem("p_ready"), sem("pt_ready")
        rx_ready, att_ready = sem("rx_ready"), sem("att_ready")
        sum_ready, rsub_ready, rexp_ready = sem("sum_ready"), sem("rsub_ready"), sem("rexp_ready")
        comb_ready, combt_ready = sem("comb_ready"), sem("combt_ready")
        acc_ready, hg_ready, out_ready = sem("acc_ready"), sem("hg_ready"), sem("out_ready")
        fences = {e: sem(f"fence_{e}") for e in ("DVE", "Pool", "SP")}
        dve_a1, dve_a2, dve_b = sem("dve_a1"), sem("dve_a2"), sem("dve_b")

        table_rows = table.rearrange("(t p) f -> p t f", p=128)
        ident = w("ident")

        def fence(engine):
            engine.sem_inc(fences[engine.engine.name], 1)

        block = ctx.enter_context(nc.Block())

        @block.sync
        def _(sp):
            def load_x(m):
                sp.dma_start(X[:], x_by_window[bass.ds(m, 1)].rearrange("a c n -> (a c) n")).then_inc(x_in, 16)

            def load_raster(m):
                if not (isinstance(m, int) and m == 0):
                    sp.wait_ge(x1_ready, m)
                sp.dma_start(XLEPE[:], x[bass.ds(m, 1)].rearrange("a c n -> (a c) n")).then_inc(raster_in, 16)

            def x_is_free(m):
                for h in range(2):
                    sp.wait_ge(a_ready[RING_A.slot(("v", h))], RING_A.turn(("v", h), m - 1))
                sp.wait_ge(xsum_ready, m)

            def store_table(m):
                sp.wait_ge(kv_ready, m + 1)
                fence(sp)
                for t in range(WTILES):
                    if not (isinstance(m, int) and m == 0):
                        sp.wait_ge(kvsel_in[t], 16 * SLOTS * m)
                sp.dma_start(table_rows, KV[:].rearrange("p t x c -> p t (x c)")).then_inc(table_in, 16)

            def store_out(n):
                sp.wait_ge(out_ready, n + 1)
                sp.dma_start(out[bass.ds(n, 1)].rearrange("a (t p) c -> p (a t) c", p=128), ACC).then_inc(out_done, 16)

            def shift_h1(n):
                for g in range(GROUPS):
                    b = g % 2
                    sp.wait_ge(h1_ready, GROUPS * n + g + 1)
                    fence(sp)
                    if g >= 2:
                        before = ("dw", g - 2)
                        sp.wait_ge(b_ready[RING_B.slot(before)], RING_B.turn(before, n))
                    rows = H1_PAD[:, b].rearrange("c y x -> c (y x)")
                    for dx in range(3):
                        sp.dma_start(SHIFTED[32 * dx:32 * dx + 32, b, :, 0:PLANE - 2], rows[:, dx:dx + PLANE - 2]
                                     ).then_inc(shifted_in[b], 16)

            def front_loads(m):
                load_raster(m)
                store_table(m)

            sp.dma_start(W[:], packed).then_inc(weights_in, 16)
            sp.dma_start(PROD[:, 0:512 + DIAGONALS + 32], gains).then_inc(weights_in, 16)
            load_x(0)
            front_loads(0)
            x_is_free(1)
            load_x(1)
            front_loads(1)
            x_is_free(2)
            load_x(2)
            with sp.Fori(0, IMAGES - 3) as n:
                shift_h1(n)
                front_loads(n + 2)
                x_is_free(n + 3)
                load_x(n + 3)
                store_out(n)
                fence(sp)
            shift_h1(IMAGES - 3)
            front_loads(IMAGES - 1)
            store_out(IMAGES - 3)
            for n in (IMAGES - 2, IMAGES - 1):
                shift_h1(n)
                store_out(n)
            sp.wait_ge(out_done, 16 * (IMAGES + 1))

        @block.tensor
        def _(pe):
            def two_halves(ps, lhs, rhs, **kw):
                for h in range(2):
                    mm = pe.matmul(ps[:, h * HALF:(h + 1) * HALF], lhs, rhs[:, h * HALF:(h + 1) * HALF], **kw)
                return mm

            whole = dict(start=True, stop=True)

            def open_a(name, m):
                s = RING_A.slot(name)
                pe.wait_ge(a_free[s], RING_A.turn(name, m))
                return psA[s], a_ready[s]

            def a_project(m, t, p):
                if t == 0 and p == 0:
                    pe.wait_ge(x_in, 16 * (m + 1))
                ps, done = open_a(("qkv", t, p), m)
                at = p * WINS + t * 128
                pe.matmul(ps[:, 0:384], X[:, at:at + 128], w("wqkv"), **whole).then_inc(done, 1)

            def a_values(m, h):
                ps, done = open_a(("v", h), m)
                pe.matmul(ps[:], w("wqkv", 256, 384), X[:, h * HALF:(h + 1) * HALF], **whole).then_inc(done, 1)

            def a_windows(m):
                pe.wait_ge(xsum_ready, m + 1)
                ps, done = open_a("windows", m)
                pe.matmul(ps[:, 0:WINS], w("wqkv", 0, 128), X_SUM4, **whole)
                pe.matmul(ps[:, WINS:2 * WINS], w("wqkv", 128, 256), X_SUM4, **whole).then_inc(done, 1)

            def a_logits(m):
                pe.wait_ge(win_ready, 2 * (m + 1))
                ps, done = open_a("logits", m)
                for t in range(WTILES):
                    mm = pe.matmul(ps[:, t * WINS:(t + 1) * WINS], QWIN[:, t * 128:(t + 1) * 128], KWIN, **whole)
                mm.then_inc(done, 1)

            def a_attended(m):
                for t in range(WTILES):
                    pe.wait_ge(attended_ready, WTILES * m + t + 1)
                    ps, done = open_a(("attended", t), m)
                    for p in range(PX):
                        mm = pe.transpose(ps[:, p * 128:(p + 1) * 128], Q[:, t, p, :], ident)
                    mm.then_inc(done, 1)

            def a_first_half(m):
                for t in range(WTILES):
                    for p in range(PX):
                        a_project(m, t, p)
                for h in range(2):
                    a_values(m, h)
                a_windows(m)
                a_logits(m)

            def emit(name, n):
                s = RING_B.slot(name)
                ps = psB[s]
                kind, i = name if isinstance(name, tuple) else (name, 0)
                if kind == "fc1" and i == 0:
                    pe.wait_ge(x1_ready, n + 1)
                if kind == "dw":
                    pe.wait_ge(shifted_in[i % 2], 16 * 3 * (2 * n + i // 2 + 1))
                if kind == "fc2":
                    pe.wait_ge(h2_ready, GROUPS * (n + 1))
                if kind == "mean":
                    pe.wait_ge(x2_ready, 2 * n + i + 1)
                if kind == "var":
                    pe.wait_ge(square_ready, 2 * n + i + 1)
                if kind == "rstd":
                    pe.wait_ge(rstd_ready, 2 * n + i + 1)
                if kind in ("v", "router"):
                    pe.wait_ge(norm_ready, 2 * n + (kind == "router") + 1)
                if kind == "scores" and i < HEADS_C:
                    pe.wait_ge(qk_ready, 2 * (HEADS_C * n + i + 1))
                if kind == "turned":
                    pe.wait_ge(p_ready, UNITS * n + i + 1)
                if kind == "wo":
                    pe.wait_ge(att_ready, TT * (n + 1))
                if kind == "combine":
                    pe.wait_ge(comb_ready, n + 1)
                if kind == "start":
                    pe.wait_ge(combt_ready, n + 1)
                    pe.wait_ge(sum_ready, n + 1)
                if kind == "expert":
                    pe.wait_ge(hg_ready, EXPERTS * n + i + 1)
                pe.wait_ge(b_free[s], RING_B.turn(name, n))
                if kind == "fc1":
                    mm = two_halves(ps, w("fc1", 128 * i, 128 * i + 128), XR, **whole)
                elif kind == "dw":
                    for dy in range(3):
                        for h in range(2):
                            for q in range(4):
                                rows = SHIFTED[:, i % 2, q].rearrange("p (y x) -> p y x", y=MSIDE)[
                                    :, 16 * h + dy:16 * h + dy + 16, 0:SIDE]
                                mm = pe.matmul(ps[32 * q:32 * q + 32, h * HALF:(h + 1) * HALF],
                                               DIAG[:, 3 * (4 * i + q) + dy, :], rows, start=dy == 0, stop=dy == 2)
                elif kind == "fc2":
                    for g in range(GROUPS):
                        mm = two_halves(ps, w("fc2", 128 * g, 128 * g + 128), H2[:, g, :],
                                        start=g == 0, stop=g == GROUPS - 1)
                elif kind == "mean":
                    mm = two_halves(ps, w("mean_w"), XR, **whole)
                elif kind == "var":
                    for t in range(TT):
                        mm = pe.matmul(ps[:, t:t + 1], SQ[:, t * 128:(t + 1) * 128], w("mean_w", 0, 1), **whole)
                elif kind == "rstd":
                    for t in range(TT):
                        mm = pe.transpose(ps[:, t * 128:(t + 1) * 128], SQ[:, t * 128:(t + 1) * 128], ident)
                elif kind in ("q", "k"):
                    mm = two_halves(ps[0:96], w("attn_" + kind, 96 * i, 96 * i + 96), TN, **whole)
                elif kind == "wo":
                    mm = two_halves(ps, w("attn_vo", 128, 256), ATT, **whole)
                elif kind == "v":
                    for t in range(TT):
                        mm = pe.matmul(ps[:, t * 128:(t + 1) * 128], TN[:, t * 128:(t + 1) * 128],
                                       w("attn_vo", 0, 128), **whole)
                elif kind == "scores":
                    q, h = divmod(i, HEADS_C)
                    mm = two_halves(ps, QS[0:96, h, q * 128:(q + 1) * 128].bitcast(F32R),
                                    KS[0:96, h].bitcast(F32R), **whole)
                elif kind == "turned":
                    for t in range(TT):
                        mm = pe.transpose(ps[:, t * 128:(t + 1) * 128], P[:, i % P_BUFFERS, t * 128:(t + 1) * 128], ident)
                elif kind == "router":
                    for t in range(TT):
                        mm = pe.matmul(ps[:, t * EXPERTS:(t + 1) * EXPERTS], TN[:, t * 128:(t + 1) * 128],
                                       w("router"), **whole)
                elif kind == "combine":
                    for t in range(TT):
                        mm = pe.transpose(ps[0:EXPERTS, t * 128:(t + 1) * 128], COMB[:, t, :], ident)
                elif kind == "start":
                    for t in range(TT):
                        cols = slice(t * 128, (t + 1) * 128)
                        pe.matmul(ps[:, cols], XR[:, cols], ident, start=True, stop=False)
                        mm = pe.matmul(ps[:, cols], COMB_T[:, cols], w("b2")[0:EXPERTS], start=False, stop=True)
                elif kind == "hidden":
                    mm = two_halves(ps, w("w1", 128 * i, 128 * i + 128), TN, **whole)
                elif kind == "expert":
                    for t in range(TT):
                        mm = pe.matmul(ps[:, t * 128:(t + 1) * 128], HG[:, i % 2, t * 128:(t + 1) * 128],
                                       w("w2", 128 * i, 128 * i + 128), **whole)
                mm.then_inc(b_ready[s], 1)

            def times_values(c, part, n):
                s = RING_A.slot(("pv", c))
                if part == 0:
                    if c == 0:
                        pe.wait_ge(vt_ready, n + 1)
                    pe.wait_ge(pt_ready, UNITS * n + HEADS_C * (c + 1))
                    pe.wait_ge(a_free[s], RING_A.turn(("pv", c), n))
                for t in range(part * TT // HEADS_C, (part + 1) * TT // HEADS_C):
                    for h in range(HEADS_C):
                        rows = slice(CH_C * h, CH_C * (h + 1))
                        pe.matmul(psA[s][rows, 0:128], V[:, t, rows], PT[:, (HEADS_C * c + h) % TURNED_BUFFERS, t, :],
                                  start=t == 0, stop=t == TT - 1)
                if part == HEADS_C - 1:
                    pe.wait_ge(rx_ready, TT * n + c + 1)
                    pe.transpose(psA[s][:, 128:256], RX[:, c % 2].rearrange("p h c -> p (h c)"), ident
                                 ).then_inc(a_ready[s], 1)

            def behind(u, n):
                c, part = divmod(u, HEADS_C)
                if c > 0:
                    times_values(c - 1, part, n)

            def stages_b_to_d(n, second, first):
                for name in ORDER_B:
                    emit(name, n)
                    if name[0] == "scores" and name[1] >= AHEAD:
                        behind(name[1] - AHEAD, n)
                    if name[0] == "turned" and name[1] + AHEAD >= UNITS:
                        behind(name[1], n)
                    if name == ("turned", UNITS - 1):
                        for part in range(HEADS_C):
                            times_values(TT - 1, part, n)
                    if second is not None and name == ("mean", 1):
                        a_attended(second)
                    if first is not None:
                        m = first
                        if name == ("var", 1):
                            for p in range(PX):
                                a_project(m, 0, p)
                        if name == ("rstd", 1):
                            for p in range(PX):
                                a_project(m, 1, p)
                        if name == "router":
                            for h in range(2):
                                a_values(m, h)
                            a_windows(m)
                        if name == ("hidden", 1):
                            a_logits(m)

            pe.wait_ge(weights_in, 32)
            pe.wait_ge(ready, 3)
            a_first_half(0)
            a_attended(0)
            a_first_half(1)
            with pe.Fori(0, IMAGES - 2) as n:
                stages_b_to_d(n, n + 1, n + 2)
            stages_b_to_d(IMAGES - 2, IMAGES - 1, None)
            stages_b_to_d(IMAGES - 1, None, None)

        @block.scalar
        def _(act):
            def a_values(m):
                if not (isinstance(m, int) and m == 0):
                    act.wait_ge(lepe_done, TAPS5 * m)
                for hy in range(2):
                    s = RING_A.slot(("v", hy))
                    act.wait_ge(a_ready[s], RING_A.turn(("v", hy), m))
                    for wx in range(2):
                        act.activation(V_PAD[:, 2 + hy:2 + hy + SIDE:2, 2 + wx:2 + wx + SIDE:2],
                                       psA[s][:, wx * WINS:(wx + 1) * WINS].rearrange("c (j i) -> c j i", i=WIN_SIDE),
                                       ACT.Identity, bias=col("bv_a")).then_inc(v_ready, 1)
                    act.wait_ge(v_ready, PX * m + 2 * hy + 2)
                    act.sem_inc(a_free[s], 1)

            def a_windows(m):
                s = RING_A.slot("windows")
                act.wait_ge(a_ready[s], RING_A.turn("windows", m))
                for i, (out, bias) in enumerate(((QWIN, "bq_a"), (KWIN, "bk_a"))):
                    act.activation(out, psA[s][:, i * WINS:(i + 1) * WINS], ACT.Identity, bias=col(bias),
                                   scale=1.0 / PX).then_inc(win_ready, 1)
                act.wait_ge(win_ready, 2 * (m + 1))
                act.sem_inc(a_free[s], 1)

            def a_exp(t, m):
                act.wait_ge(s_ready, WTILES * m + t + 1)
                act.activation(S[:], S[:], ACT.Exp, scale=SCALE_A).then_inc(e_ready, 1)

            def evacuate(name, n, signal, *ops):
                s = RING_B.slot(name)
                act.wait_ge(b_ready[s], RING_B.turn(name, n))
                for op in ops[:-1]:
                    op(psB[s])
                ops[-1](psB[s]).then_inc(b_free[s], 1)
                act.wait_ge(b_free[s], RING_B.turn(name, n) + 1)
                act.sem_inc(signal, 1)

            def fc1(g, n):
                if g >= 2:
                    act.wait_ge(shifted_in[g % 2], 16 * 3 * (2 * n + 1))
                evacuate(("fc1", g), n, h1_ready, lambda ps: act.activation(
                    H1_PAD[:, g % 2, 1:1 + SIDE, 1:1 + SIDE], ps[:].rearrange("c (y x) -> c y x", y=SIDE),
                    ACT.Identity, bias=col("b_fc1", g), scale=col("g_fc1", g)))

            def dw(g, n):
                evacuate(("dw", g), n, h2_ready, lambda ps: act.activation(
                    H2[:, g, :], ps[:], ACT.Relu, bias=col("b_dw", g)))

            def norm(i, n):
                act.wait_ge(centred_ready, 2 * n + i + 1)
                act.activation(SQ[:], TN[:], ACT.Square).then_inc(square_ready, 1)
                evacuate(("var", i), n, std_ready, lambda ps: act.activation(
                    STD[:], ps[:, 0:TT], ACT.Sqrt, bias=col("eps")))

            def exp(u, n):
                act.wait_ge(scaled_ready, UNITS * n + u + 1)
                q, h = divmod(u, HEADS_C)
                b = u % P_BUFFERS
                act.activation(P[:, b, :], P[:, b, :], ACT.Exp, bias=NEGMAX[:, b, 1:2],
                               accum_out=L[:, q, h:h + 1]).then_inc(p_ready, 1)

            def turned(u, n):
                if u == GROUPS:
                    act.wait_ge(out_done, 16 * (n + 1))
                evacuate(("turned", u), n, pt_ready, lambda ps: act.activation(
                    PT[:, u % TURNED_BUFFERS].rearrange("k t q -> k (t q)"), ps[:], ACT.Copy))

            def stages_b_to_d(n, second, first):
                fc1(0, n)
                fc1(1, n)
                dw(0, n)
                fc1(2, n)
                if second is not None:
                    a_exp(0, second)
                dw(1, n)
                fc1(3, n)
                dw(2, n)
                dw(3, n)
                norm(0, n)
                for h in range(HEADS_C):
                    for kind, stacked in (("q", QS), ("k", KS)):
                        s = RING_B.slot((kind, h))
                        act.wait_ge(b_ready[s], RING_B.turn((kind, h), n))
                        act.activation(stacked[0:96, h].bitcast(F32R), psB[s][0:96, :], ACT.Identity,
                                       bias=col(f"b{kind}_c", h)[0:96]).then_inc(high_ready, 1)
                exp(0, n)
                for u in range(UNITS):
                    if u + 1 < UNITS:
                        exp(u + 1, n)
                    turned(u, n)
                    if second is not None and u == 14:
                        a_exp(1, second)
                norm(1, n)
                act.wait_ge(rsub_ready, n + 1)
                act.activation(PROBS, PROBS, ACT.Exp).then_inc(rexp_ready, 1)

                def gelu(e):
                    evacuate(("hidden", e), n, hg_ready, lambda ps: act.activation(
                        HG[:, e % 2, :], ps[:], ACT.Gelu, bias=col("b1", e)))

                if first is not None:
                    a_values(first)
                    a_windows(first)
                gelu(0)
                gelu(1)
                evacuate("combine", n, combt_ready, lambda ps: act.activation(COMB_T[:], ps[0:EXPERTS, :], ACT.Copy))
                evacuate("start", n, acc_ready, lambda ps: act.activation(
                    ACC.rearrange("p t c -> p (t c)"), ps[:], ACT.Copy))
                for e in range(2, EXPERTS):
                    gelu(e)

            act.wait_ge(weights_in, 32)
            act.wait_ge(ready, 3)
            a_values(0)
            a_windows(0)
            a_exp(0, 0)
            a_exp(1, 0)
            a_values(1)
            a_windows(1)
            with act.Fori(0, IMAGES - 2) as n:
                stages_b_to_d(n, n + 1, n + 2)
            stages_b_to_d(IMAGES - 2, IMAGES - 1, None)
            stages_b_to_d(IMAGES - 1, None, None)

        @block.vector
        def _(dve):
            class Chain:

                def __init__(self, counter, per_image):
                    self.counter, self.per_image = counter, per_image

                def at_image(self, n):
                    self.base, self.k = n * self.per_image, 0

                def mark(self, ins):
                    self.k += 1
                    ins.then_inc(self.counter, 1)

                def settle(self):
                    if self.k:
                        dve.wait_ge(self.counter, self.base + self.k)

                def link(self, ins):
                    self.mark(ins)
                    self.settle()

                def check(self):
                    assert self.k == self.per_image, (self.counter, self.k)

            first_chain, second_chain, chain_b = Chain(dve_a1, LINKS_A1), Chain(dve_a2, LINKS_A2), Chain(dve_b, LINKS_B)

            def first_half(m):
                chain = first_chain

                def sums():
                    chain.at_image(m)
                    dve.wait_ge(x_in, 16 * (m + 1))
                    dve.tensor_reduce(X_SUM4, X[:].rearrange("c (p w) -> c w p", p=PX), AX.X,
                                      ALU.add).then_inc(xsum_ready, 1)

                def rows(t, p):
                    if t == 0 and p == 0 and not (isinstance(m, int) and m == 0):
                        dve.wait_ge(table_in, 16 * m)
                        dve.wait_ge(lepe_done, TAPS5 * m)
                    s = RING_A.slot(("qkv", t, p))
                    dve.wait_ge(a_ready[s], RING_A.turn(("qkv", t, p), m))
                    bias = w("qkv_bias")
                    chain.mark(dve.tensor_tensor(Q[:, t, p, :], psA[s][:, 0:128], bias[:, 0:128], ALU.add))
                    chain.mark(dve.tensor_tensor(KV[:, t, p, :], psA[s][:, 128:384], bias[:, 128:384], ALU.add))
                    chain.settle()
                    dve.sem_inc(a_free[s], 1)
                    if t == WTILES - 1 and p == PX - 1:
                        dve.sem_inc(kv_ready, 1)

                def choose():
                    s = RING_A.slot("logits")
                    dve.wait_ge(a_ready[s], RING_A.turn("logits", m))
                    fence(dve)
                    for t in range(WTILES):
                        chain.mark(dve.max(TOP[:, t, :], psA[s][:, t * WINS:(t + 1) * WINS]))
                    chain.settle()
                    fence(dve)
                    for t in range(WTILES):
                        chain.mark(dve.max_index(CHOSEN[:, t, :], TOP[:, t, :], psA[s][:, t * WINS:(t + 1) * WINS]))
                    chain.settle()
                    dve.sem_inc(a_free[s], 1)
                    dve.sem_inc(chosen_ready, 1)
                    chain.check()

                return [sums] + [lambda t=t, p=p: rows(t, p) for t in range(WTILES) for p in range(PX)] + [choose]

            def second_half(m):
                chain = second_chain

                def multiply_keys(t, q):
                    if t == 0 and q == 0:
                        chain.at_image(m)
                    if q == 0:
                        dve.wait_ge(kvsel_in[t], 16 * SLOTS * (m + 1))
                    chain.settle()
                    chain.mark(dve.tensor_tensor(PROD[:].rearrange("p (k c) -> p k c", k=KEYS), KVSEL[:, t, :, 0:C],
                                                 Q[:, t, q, :].unsqueeze(1).broadcast_to([128, KEYS, C]), ALU.mult))

                def sum_channels(t, q):
                    chain.settle()
                    chain.mark(dve.tensor_reduce(S[:, q].rearrange("p k h -> p (k h)"),
                                                 PROD[:].rearrange("p (k c) -> p k c", c=CH_A), AX.X, ALU.add))

                def less_maximum(t):
                    top, by_head = SUMS[:, 0, :], S[:].rearrange("p q k h -> p q h k")
                    chain.settle()
                    chain.link(dve.tensor_reduce(top.rearrange("p (q h) -> p q h", q=PX), by_head, AX.X, ALU.max))
                    dve.tensor_tensor(S[:], S[:], top.rearrange("p (q h) -> p q h", q=PX).unsqueeze(2)
                                      .broadcast_to([128, PX, KEYS, HEADS_A]), ALU.subtract).then_inc(s_ready, 1)

                def sum_keys(t):
                    dve.wait_ge(e_ready, WTILES * m + t + 1)
                    chain.link(dve.tensor_reduce(SUMS[:, 0, :].rearrange("p (q h) -> p q h", q=PX),
                                                 S[:].rearrange("p q k h -> p q h k"), AX.X, ALU.add))
                    chain.mark(dve.reciprocal(SUMS[:, 1, :], SUMS[:, 0, :]))

                def multiply_values(t, q):
                    chain.settle()
                    chain.mark(dve.tensor_tensor(PROD[:].rearrange("p (k h c) -> p k h c", k=KEYS, h=HEADS_A),
                                                 KVSEL[:, t, :, C:2 * C].rearrange("p k (h c) -> p k h c", h=HEADS_A),
                                                 S[:, q].unsqueeze(3).broadcast_to([128, KEYS, HEADS_A, CH_A]),
                                                 ALU.mult))

                def attend(t, q):
                    chain.settle()
                    chain.mark(dve.tensor_reduce(Q[:, t, q, :], PROD[:].rearrange("p (k f) -> p f k", k=KEYS),
                                                 AX.X, ALU.add))
                    if q == PX - 1:
                        chain.settle()
                        dve.sem_inc(pv_done, 1)
                        heads = Q[:, t].rearrange("p q (h c) -> p (q h) c", h=HEADS_A)
                        dve.tensor_tensor(heads, heads, SUMS[:, 1, :].unsqueeze(2)
                                          .broadcast_to([128, PX * HEADS_A, CH_A]), ALU.mult).then_inc(attended_ready, 1)

                steps = []
                for t in range(WTILES):
                    for q in range(PX):
                        steps += [lambda t=t, q=q: multiply_keys(t, q), lambda t=t, q=q: sum_channels(t, q)]
                    steps += [lambda t=t: less_maximum(t), lambda t=t: sum_keys(t)]
                    for q in range(PX):
                        steps += [lambda t=t, q=q: multiply_values(t, q), lambda t=t, q=q: attend(t, q)]
                return steps

            def window_residual(m):
                dve.wait_ge(lepe_done, TAPS5 * (m + 1))
                dims = dict(j=WIN_SIDE, hy=2, i=WIN_SIDE, wx=2)
                for t in range(WTILES):
                    s = RING_A.slot(("attended", t))
                    dve.wait_ge(a_ready[s], RING_A.turn(("attended", t), m))
                    for p in range(PX):
                        hy, wx = divmod(p, 2)
                        place = XLEPE[:].rearrange("c (j hy i wx) -> c hy j i wx", **dims)[:, hy, 8 * t:8 * t + 8, :, wx]
                        second_chain.mark(dve.scalar_tensor_tensor(
                            out=place, in0=psA[s][:, p * 128:(p + 1) * 128].rearrange("c (j i) -> c j i", j=8),
                            scalar=col("b_lepe"), in1=place, op0=ALU.add, op1=ALU.add))
                    second_chain.settle()
                    dve.sem_inc(a_free[s], 1)

            def to_stream(m):
                if not (isinstance(m, int) and m == 0):
                    s = RING_B.slot("start")
                    dve.wait_ge(b_ready[s], RING_B.turn("start", m - 1))
                dve.tensor_copy(XR[:], XLEPE[:]).then_inc(x1_ready, 1)
                second_chain.check()

            def stages_b_to_d(n, second, first):
                link = chain_b.link
                chain_b.at_image(n)
                steps = second_half(second) if second is not None else []
                front = first_half(first) if first is not None else []

                def run(queue, count):
                    for _ in range(min(count, len(queue))):
                        queue.pop(0)()

                def arrived(name):
                    s = RING_B.slot(name)
                    dve.wait_ge(b_ready[s], RING_B.turn(name, n))
                    return psB[s], b_free[s]

                def residual_add(name, bias):
                    ps, free = arrived(name)
                    link(dve.scalar_tensor_tensor(out=XR[:], in0=ps[:], scalar=bias, in1=XR[:],
                                                  op0=ALU.add, op1=ALU.add))
                    dve.sem_inc(free, 1)
                    dve.sem_inc(x2_ready, 1)

                def centre(i):
                    ps, free = arrived(("mean", i))
                    link(dve.tensor_tensor(TN[:], XR[:], ps[:], ALU.subtract))
                    dve.sem_inc(free, 1)
                    dve.sem_inc(centred_ready, 1)

                def normalise(i, between=None):
                    dve.wait_ge(std_ready, 2 * n + i + 1)
                    link(dve.reciprocal(STD[:], STD[:]))
                    dve.tensor_copy(SQ[:].rearrange("p (t c) -> p t c", t=TT), STD[:].unsqueeze(2)
                                    .broadcast_to([128, TT, C])).then_inc(rstd_ready, 1)
                    if between:
                        between()
                    ps, free = arrived(("rstd", i))
                    link(dve.tensor_tensor(TN[:], TN[:], ps[:], ALU.mult))
                    dve.sem_inc(free, 1)
                    dve.sem_inc(norm_ready, 1)

                def scale_scores(u):
                    ps, free = arrived(("scores", u))
                    b = u % P_BUFFERS
                    at = TOK - 128 - 128 * (u // HEADS_C)
                    fence(dve)
                    dve.tensor_tensor_reduce(P[:, b, :], ps[:], w("band", at, at + TOK), 1.0, -3.0e38,
                                             ALU.mult, ALU.max, NEGMAX[:, b, 0:1]).then_inc(free, 1)
                    if u > 0:
                        negate_maximum(u - 1)

                def negate_maximum(u):
                    s, b = RING_B.slot(("scores", u)), u % P_BUFFERS
                    dve.wait_ge(b_free[s], RING_B.turn(("scores", u), n) + 1)
                    dve.tensor_scalar(NEGMAX[:, b, 1:2], NEGMAX[:, b, 0:1], -1.0, None,
                                      ALU.mult).then_inc(scaled_ready, 1)

                def normaliser(c):
                    dve.wait_ge(p_ready, UNITS * n + HEADS_C * (c + 1))
                    link(dve.reciprocal(L[:, c, :], L[:, c, :]))
                    dve.tensor_copy(RX[:, c % 2], L[:, c, :].unsqueeze(2).broadcast_to([128, HEADS_C, CH_C])
                                    ).then_inc(rx_ready, 1)

                def attended(c):
                    s = RING_A.slot(("pv", c))
                    dve.wait_ge(a_ready[s], RING_A.turn(("pv", c), n))
                    link(dve.tensor_copy(RT, psA[s][:, 128:256]))
                    link(dve.tensor_tensor(ATT[:, 128 * c:128 * (c + 1)], psA[s][:, 0:128], RT, ALU.mult))
                    dve.sem_inc(a_free[s], 1)
                    dve.sem_inc(att_ready, 1)

                run(steps, 18)
                residual_add("fc2", col("b_fc2"))
                centre(0)
                run(steps, 1)
                normalise(0)
                run(steps, 1)
                ps, free = arrived("v")
                link(dve.tensor_tensor(V[:], ps[:].rearrange("p (t c) -> p t c", t=TT),
                                       w("bv_row").unsqueeze(1).broadcast_to([128, TT, C]), ALU.add))
                dve.sem_inc(free, 1)
                dve.sem_inc(vt_ready, 1)
                for h in range(HEADS_C):
                    for j, (kind, stacked, rows) in enumerate((("q", QS, slice(64, 96)), ("k", KS, slice(32, 64)))):
                        ps, free = arrived((kind, h))
                        dve.wait_ge(high_ready, 2 * (HEADS_C * n + h) + j + 1)
                        link(dve.scalar_tensor_tensor(out=stacked[rows, h].bitcast(F32R), in0=ps[rows, :],
                                                      scalar=col(f"b{kind}_c", h)[rows], in1=stacked[rows, h],
                                                      op0=ALU.add, op1=ALU.subtract))
                        dve.sem_inc(free, 1)
                        dve.sem_inc(qk_ready, 1)
                    if h > 0:
                        scale_scores(h - 1)
                for u in range(HEADS_C - 1, UNITS):
                    scale_scores(u)
                    if u % 2 == 1:
                        run(steps, 1)
                    if u % HEADS_C == 2 and u >= HEADS_C:
                        normaliser(u // HEADS_C - 1)
                    if u % HEADS_C == HEADS_C - 1 and u >= 2 * HEADS_C:
                        attended(u // HEADS_C - 2)
                negate_maximum(UNITS - 1)
                run(steps, 16)
                normaliser(TT - 1)
                attended(TT - 2)
                attended(TT - 1)
                assert not steps
                residual_add("wo", col("bo_c"))
                centre(1)
                if second is not None:
                    window_residual(second)
                run(front, 2)
                normalise(1, lambda: run(front, 4))
                dve.tensor_tensor(XR[:], XR[:], TN[:], ALU.add).then_inc(sum_ready, 1)
                run(front, 3)
                ps, free = arrived("router")
                logits = ps[:, 0:TT * EXPERTS].rearrange("p (t e) -> p t e", t=TT)
                over_e = [128, TT, EXPERTS]
                link(dve.tensor_reduce(RSTAT[:, 0, :], logits, AX.X, ALU.max))
                link(dve.tensor_tensor(PROBS, logits, RSTAT[:, 0, :].unsqueeze(2).broadcast_to(over_e), ALU.subtract))
                dve.sem_inc(free, 1)
                dve.sem_inc(rsub_ready, 1)
                dve.wait_ge(rexp_ready, n + 1)
                link(dve.tensor_reduce(RSTAT[:, 1, :], PROBS, AX.X, ALU.add))
                link(dve.reciprocal(RSTAT[:, 2, :], RSTAT[:, 1, :]))
                link(dve.tensor_tensor(PROBS, PROBS, RSTAT[:, 2, :].unsqueeze(2).broadcast_to(over_e), ALU.mult))
                fence(dve)
                for t in range(TT):
                    last = dve.max(BEST[:, t, :], PROBS[:, t, :])
                link(last)
                fence(dve)
                for t in range(TT):
                    last = dve.max_index(BEST_AT[:, t, :], BEST[:, t, :], PROBS[:, t, :])
                link(last)
                link(dve.tensor_tensor(RSTAT[:, 0, :], BEST[:, :, 0], BEST[:, :, 1], ALU.add))
                link(dve.tensor_scalar(RSTAT[:, 1, :], RSTAT[:, 0, :], 1e-12, None, ALU.max))
                link(dve.reciprocal(RSTAT[:, 2, :], RSTAT[:, 1, :]))
                dve.tensor_tensor(BEST_W, BEST[:, :, 0:2], RSTAT[:, 2, :].unsqueeze(2).broadcast_to([128, TT, 2]), ALU.mult)
                link(dve.tensor_copy(BEST_ATF, BEST_AT[:, :, 0:2]))
                iota = w("iota").rearrange("p (t e) -> p t e", t=TT)
                for k in range(2):
                    last = dve.tensor_tensor(PICK[:, k], iota, BEST_ATF[:, :, k:k + 1].broadcast_to(over_e), ALU.is_equal)
                link(last)
                for k in range(2):
                    last = dve.tensor_tensor(PICK[:, k], PICK[:, k], BEST_W[:, :, k:k + 1].broadcast_to(over_e), ALU.mult)
                link(last)
                link(dve.tensor_tensor(COMB, PICK[:, 0], PICK[:, 1], ALU.add))
                dve.sem_inc(comb_ready, 1)
                run(front, 1)
                dve.wait_ge(acc_ready, n + 1)
                for e in range(EXPERTS):
                    ps, free = arrived(("expert", e))
                    for t in range(TT):
                        last = dve.scalar_tensor_tensor(out=ACC[:, t, :], in0=ps[:, t * 128:(t + 1) * 128],
                                                        scalar=COMB[:, t, e:e + 1], in1=ACC[:, t, :],
                                                        op0=ALU.mult, op1=ALU.add)
                    link(last)
                    dve.sem_inc(free, 1)
                    if e == 0 and second is not None:
                        to_stream(second)
                dve.sem_inc(out_ready, 1)
                chain_b.check()

            dve.wait_ge(weights_in, 32)
            dve.tensor_tensor(w("wqkv"), w("wqkv"), PROD[:, 0:384], ALU.mult)
            for g in range(GROUPS):
                wg = w("fc2", 128 * g, 128 * g + 128)
                dve.tensor_tensor(wg, wg, PROD[:, 384:512], ALU.mult)
            shape = [128, DIAGONALS, 32]
            taps, eye = PROD[:, 512:512 + DIAGONALS], PROD[:, 512 + DIAGONALS:512 + DIAGONALS + 32]
            dve.tensor_tensor(DIAG[:], eye.unsqueeze(1).broadcast_to(shape), taps.unsqueeze(2).broadcast_to(shape),
                              ALU.mult).then_inc(ready, 1)
            dve.wait_ge(ready, 3)
            for step in first_half(0) + second_half(0):
                step()
            window_residual(0)
            to_stream(0)
            for step in first_half(1):
                step()
            with dve.Fori(0, IMAGES - 2) as n:
                stages_b_to_d(n, n + 1, n + 2)
            stages_b_to_d(IMAGES - 2, IMAGES - 1, None)
            stages_b_to_d(IMAGES - 1, None, None)

        @block.gpsimd
        def _(pool):
            def gathers(m):
                pool.wait_ge(chosen_ready, m + 1)
                pool.wait_ge(table_in, 16 * (m + 1))
                if not (isinstance(m, int) and m == 0):
                    pool.wait_ge(pv_done, WTILES * m)
                fence(pool)
                for t in range(WTILES):
                    for s in range(SLOTS):
                        pool.indirect_dma_start(
                            KVSEL[:, t, PX * s:PX * (s + 1), :].rearrange("p x c -> p (x c)"), None, table,
                            bass.IndirectOffsetOnAxis(ap=CHOSEN[:, t, s:s + 1], axis=0)).then_inc(kvsel_in[t], 16)

            def taps(m):
                pool.wait_ge(raster_in, 16 * (m + 1))
                pool.wait_ge(v_ready, PX * (m + 1))
                acc = XLEPE[:].rearrange("c (y x) -> c y x", y=SIDE)
                product = TAP.rearrange("c (y x) -> c y x", y=SIDE)
                for tap in range(TAPS5):
                    dy, dx = divmod(tap, 5)
                    fence(pool)
                    pool.tensor_scalar(product, V_PAD[:, dy:dy + SIDE, dx:dx + SIDE], col("lepe_w", tap), 0.0,
                                       ALU.mult, ALU.add).then_inc(tap_ready, 1)
                    pool.wait_ge(tap_ready, TAPS5 * m + tap + 1)
                    pool.tensor_tensor(acc, acc, product, ALU.add).then_inc(lepe_done, 1)
                    pool.wait_ge(lepe_done, TAPS5 * m + tap + 1)

            pool.memset(V_PAD[:], 0.0).then_inc(ready, 1)
            pool.memset(H1_PAD[:], 0.0)
            pool.memset(STACKED[:], 0.0).then_inc(ready, 1)
            for s in range(2):
                pool.sem_inc(a_free[s], 1)
            for s in range(3):
                pool.sem_inc(b_free[s], 1)
            pool.sem_inc(out_done, 16)
            pool.wait_ge(weights_in, 32)
            gathers(0)
            taps(0)
            gathers(1)
            taps(1)
            with pool.Fori(0, IMAGES - 2) as n:
                gathers(n + 2)
                taps(n + 2)


def kernel(**inputs):
    import numpy as np
    import concourse.bacc as bacc
    from concourse.bass_utils import run_bass_kernel_spmd

    a = {k: np.asarray(v) for k, v in inputs.items()}
    f32 = np.float32

    def cols(v):
        return v.reshape(-1, 128).T

    def everywhere(v):
        return np.broadcast_to(v.reshape(1, -1), (128, v.size))

    L0 = {k[8:]: v for k, v in a.items() if k.startswith("L0_conv_")}
    L1 = {k[3:]: v for k, v in a.items() if k.startswith("L1_")}
    def thrice(m):
        rows = m.shape[0]
        return np.broadcast_to(m.reshape(rows, HEADS_C, 1, CH_C), (rows, HEADS_C, 3, CH_C)).reshape(rows, -1)

    def by_quarter(m):
        return m.transpose(0, 2, 1, 3).reshape(GROUPS, 128, -1)

    dw = np.zeros((128, DIAGONALS), f32)
    dw[:96] = L0["w_dw"].reshape(GROUPS, 32, 4, 3, 3).transpose(4, 1, 0, 2, 3).reshape(96, -1)
    eye = np.zeros((128, 32), f32)
    eye[:96] = np.tile(np.eye(32, dtype=f32), (3, 1))
    b2 = np.zeros((128, 128), f32)
    b2[:EXPERTS] = L1["ffn_b2"]
    distance = np.abs(np.arange(BAND)[None, :] - (TOK - 128) - np.arange(128)[:, None])
    band = ((TOK - distance) / TOK / np.sqrt(CH_C)).astype(f32)
    parts = {
        "wqkv": np.concatenate([L0["wq"].T, L0["wkv"].T], 1),
        "qkv_bias": everywhere(np.concatenate([L0["bq"], L0["bkv"]])),
        "fc1": L0["w_fc1"].T,
        "fc2": by_quarter(L0["w_fc2"].T.reshape(GROUPS, 32, 4, 128)).transpose(1, 0, 2).reshape(128, -1),
        "attn_q": thrice(L1["attn_Wq"]), "attn_k": thrice(L1["attn_Wk"]),
        "attn_vo": np.concatenate([L1["attn_Wv"], L1["attn_Wo"]], 1),
        "bv_row": everywhere(L1["attn_bv"]),
        "router": L1["ffn_router_w"].T,
        "w1": L1["ffn_w1"].transpose(1, 0, 2).reshape(128, -1),
        "w2": L1["ffn_w2"].transpose(1, 0, 2).reshape(128, -1),
        "b2": b2,
        "lepe_w": L0["w_lepe"].reshape(128, TAPS5),
        "bq_a": cols(L0["bq"]), "bk_a": cols(L0["bkv"][:128]), "bv_a": cols(L0["bkv"][128:]),
        "b_lepe": cols(L0["b_lepe"]), "g_fc1": cols(L0["g_fc1"]), "b_fc1": cols(L0["b_fc1"]),
        "b_dw": by_quarter(L0["b_dw"].reshape(GROUPS, 32, 4, 1))[:, :, 0].T, "b_fc2": cols(L0["b_fc2"]),
        "bq_c": thrice(L1["attn_bq"][None]).reshape(HEADS_C, 96).T, "bk_c": thrice(L1["attn_bk"][None]).reshape(HEADS_C, 96).T,
        "bo_c": cols(L1["attn_bo"]),
        "b1": L1["ffn_b1"].T,
        "ident": np.eye(128, dtype=f32),
        "mean_w": np.full((128, 128), 1.0 / 128, f32),
        "band": band,
        "iota": np.broadcast_to(np.tile(np.arange(EXPERTS, dtype=f32), TT), (128, TT * EXPERTS)),
        "eps": np.full((128, 1), LN_EPS, f32),
    }
    for name in ("bq_c", "bk_c"):
        parts[name] = np.concatenate([parts[name], np.zeros((32, HEADS_C), f32)], 0)
    for name, width in SECTIONS:
        assert parts[name].shape == (128, width), (name, parts[name].shape)
    arrays = {
        "x_dram": np.ascontiguousarray(a["x"].reshape(IMAGES, C, TOK)),
        "x_by_window_dram": np.ascontiguousarray(a["x"].reshape(IMAGES, C, WIN_SIDE, 2, WIN_SIDE, 2)
                                                 .transpose(0, 1, 3, 5, 2, 4)).reshape(IMAGES, C, TOK),
        "packed_dram": np.ascontiguousarray(np.concatenate([parts[name] for name, _ in SECTIONS], 1)),
        "gains_dram": np.ascontiguousarray(np.concatenate(
            [everywhere(np.concatenate([L0["gq"], L0["gkv"], L0["g_fc2"]])), dw, eye], 1)),
    }
    nc = bacc.Bacc("TRN2", target_bir_lowering=False, num_devices=1)
    args = [nc.dram_tensor(k, v.shape, F32, kind="ExternalInput").ap() for k, v in arrays.items()]
    out = nc.dram_tensor("out_dram", (IMAGES, TOK, C), F32, kind="ExternalOutput").ap()
    table = nc.dram_tensor("window_table", (WINS, PX * 2 * C), F32).ap()
    hybrid_layers(nc, *args, out, table)
    r = run_bass_kernel_spmd(nc, [arrays], core_ids=[0])
    got = r.results[0]["out_dram"]
    return np.ascontiguousarray(got.transpose(0, 2, 1)).reshape(IMAGES, C, SIDE, SIDE)
```

```python
from contextlib import ExitStack

import concourse.bass as bass
from concourse import mybir

F32 = mybir.dt.float32
F32R = mybir.dt.float32r
U32 = mybir.dt.uint32
ALU = mybir.AluOpType
ACT = mybir.ActivationFunctionType
AX = mybir.AxisListType

IMAGES, C, SIDE = 8, 128, 32
TOK = SIDE * SIDE
HALF = TOK // 2
WIN_SIDE = SIDE // 2
WINS = WIN_SIDE * WIN_SIDE
WTILES = WINS // 128
PX = 4
SLOTS = 4
KEYS = SLOTS * PX
HEADS_A, CH_A = 8, 16
SCALE_A = float(C) ** -0.5
LSIDE = SIDE + 4
TAPS5 = 25
GROUPS = 4
MSIDE = SIDE + 2
QUADS = GROUPS * 4
PLANE = MSIDE * MSIDE
DIAGONALS = QUADS * 3
HEADS_C, CH_C = 4, 32
TT = TOK // 128
UNITS = TT * HEADS_C
AHEAD = 3
P_BUFFERS = AHEAD
PROJECTED = 21
TURNED_BUFFERS = 2 * HEADS_C
LN_EPS = 1e-5
TABLES = 6
EXPERTS = 8
BAND = 2 * TOK - 128

SECTIONS = [("wqkv", 384), ("qkv_bias", 384), ("fc1", 512), ("fc2", 512), ("attn_q", 384), ("attn_k", 384),
            ("attn_vo", 256), ("bv_row", 128),
            ("router", EXPERTS), ("w1", 1024), ("w2", 1024), ("b2", 128), ("lepe_w", TAPS5),
            ("bq_a", 1), ("bk_a", 1), ("bv_a", 1), ("b_lepe", 1),
            ("g_fc1", GROUPS), ("b_fc1", GROUPS), ("b_dw", GROUPS), ("b_fc2", 1),
            ("bq_c", HEADS_C), ("bk_c", HEADS_C), ("bo_c", 1), ("b1", EXPERTS),
            ("ident", 128), ("centring", 128), ("mean_w", 1), ("band", BAND), ("iota", TT * EXPERTS), ("eps", 1)]
COLUMN = {}
_at = 0
for _name, _width in SECTIONS:
    COLUMN[_name] = (_at, _width)
    _at += _width
PACKED = _at


class Ring:

    def __init__(self, entries, slots):
        self.place, self.uses = {}, [0] * slots
        for i, name in enumerate(entries):
            s = i % slots
            self.place[name] = (s, self.uses[s])
            self.uses[s] += 1

    def slot(self, name):
        return self.place[name][0]

    def turn(self, name, n):
        s, k = self.place[name]
        return n * self.uses[s] + k + 1


class SharedRing(Ring):

    def __init__(self, first, middle, second, slots):
        super().__init__(first + middle + second, slots)
        self.first, self.middle = first, middle

    def turn(self, name, m):
        s, k = self.place[name]
        if name in self.middle:
            m = m + 1
        turn = m * self.uses[s] + k + 1
        if not (isinstance(m, int) and m == 0 and name in self.first):
            turn = turn - sum(self.place[other][0] == s for other in self.middle)
        if isinstance(m, int) and m == IMAGES:
            turn -= sum(self.place[other][0] == s for other in self.first)
        return turn


RING_A = SharedRing(["windows", "logits"] + [("qkv", t, p) for t in range(WTILES) for p in range(PX)] + [("v", 0), ("v", 1)],
                    [("pv", t) for t in range(TT)], [("attended", t) for t in range(WTILES)], 2)


class EarlyRing(Ring):

    def __init__(self, entries, early, slots):
        super().__init__(entries, slots)
        self.entries, self.early = entries, early

    def turn(self, name, n):
        s, k = self.place[name]
        on_slot = [other for other in self.early if self.place[other][0] == s]
        if name in self.early:
            if isinstance(n, int) and n == 0:
                return on_slot.index(name) + 1
            n = n - 1
        turn = n * self.uses[s] + k + 1 + len(on_slot)
        if isinstance(n, int) and n == IMAGES - 1:
            turn -= sum(self.entries.index(other) < self.entries.index(name) for other in on_slot)
        return turn


NEXT_IMAGE = 4


def main_order():
    order = [("fc1", 2), ("dw", 0), ("fc1", 3), ("dw", 1), ("dw", 2), ("dw", 3)]
    order += [("fc2", 0), ("fc2", 1), ("centred", 0, 0), ("centred", 0, 1), ("var", 0, 0), ("var", 0, 1),
              ("rstd", 0, 0), ("rstd", 0, 1), "v"]
    for h in range(HEADS_C):
        order.append(("q", h))
        if h == 3:
            order.append(("turned", 0))
        order.append(("k", h))
        if 0 < h:
            order.append(("scores", h - 1))
    for u in range(UNITS):
        if u > 0:
            order.append(("turned", u))
        if u + AHEAD < UNITS:
            order.append(("scores", u + AHEAD))
        order += {PROJECTED: [("wo", 0)], PROJECTED + 3: [("centred", 1, 0)]}.get(u, [])
    order += [("var", 1, 0), ("wo", 1), ("centred", 1, 1), ("rstd", 1, 0), ("var", 1, 1), ("rstd", 1, 1),
              "router", ("hidden", 0), "start", "combine", ("hidden", 1)]
    for e in range(EXPERTS):
        order.append(("expert", e))
        if e + 2 < EXPERTS:
            order.append(("hidden", e + 2))
        if e in (NEXT_IMAGE, NEXT_IMAGE + 1):
            order.append(("fc1", e - NEXT_IMAGE))
    return order


ORDER_B = main_order()
RING_B = EarlyRing(ORDER_B, [("fc1", 0), ("fc1", 1)], 3)

PROJECTIONS_AFTER = {"router": [(0, 0)], "combine": [(0, 1), (0, 2)], ("hidden", 1): [(0, 3), (1, 0)],
                     "start completed": [(1, 1), (1, 2)], ("expert", 0): [(1, 3)]}

LINKS_A1 = 20
LINKS_A2 = 30
EARLY_STEPS = 6
MLP_STEPS = 20
WINDOW_STEPS_AT = [3, 5, 8, 11, 14, 17, 19, 22, 25, 28]
STEPS_TO_SOFTMAX = 26
LINKS_B = 67


def hybrid_layers(nc, x, x_by_window, packed, gains, out, table):
    with ExitStack() as ctx:
        def sb(name, shape, dt=F32):
            return ctx.enter_context(nc.sbuf_tensor(name, shape, dt))

        def sem(name):
            return ctx.enter_context(nc.semaphore(name))

        W = sb("W", [128, PACKED])

        def w(name, a=0, b=None):
            at, width = COLUMN[name]
            return W[:, at + a:at + (width if b is None else b)]

        def col(name, i=0):
            return w(name, i, i + 1)

        X = sb("X", [128, TOK])
        Q = sb("Q", [128, WTILES, PX, C])
        KV = sb("KV", [128, WTILES, PX, 2 * C])
        V_PAD = sb("V_PAD", [128, LSIDE, LSIDE])
        KVSEL = sb("KVSEL", [128, WTILES, KEYS, 2 * C])
        PROD = sb("PROD", [128, KEYS * C])
        S = [sb("S", [128, PX, KEYS, HEADS_A])[:],
             KVSEL[:, 0, :, 0:PX * HEADS_A].rearrange("p k (q h) -> p q k h", q=PX)]
        SUMS = sb("SUMS", [128, 2, PX * HEADS_A])
        TOP = sb("TOP", [128, WTILES, 8])
        CHOSEN = sb("CHOSEN", [128, WTILES, 8], U32)
        XLEPE = sb("XLEPE", [128, TOK])
        X_SUM4, QWIN, KWIN = (PROD[:, i * WINS:(i + 1) * WINS] for i in range(3))
        TAP = KV[:, 0].rearrange("p x c -> p (x c)")
        PRODUCTS = [KV[:, i].rearrange("p x c -> p (x c)") for i in range(2)]
        XR = sb("XR", [128, TOK])
        DIAG = sb("DIAG", [128, DIAGONALS, 32])
        STACKED = sb("STACKED", [128, 2 * 4 * PLANE])
        SHIFTED = STACKED[:].rearrange("p (b q n) -> p b q n", b=2, q=4)
        QS = STACKED[:, 0:HEADS_C * TOK].rearrange("p (h n) -> p h n", h=HEADS_C)
        KS = STACKED[:, HEADS_C * TOK:2 * HEADS_C * TOK].rearrange("p (h n) -> p h n", h=HEADS_C)
        H1_PAD = sb("H1_PAD", [128, 2, MSIDE, MSIDE])
        STD = sb("STD", [128, 2, TT // 2])
        PT = sb("PT", [128, TURNED_BUFFERS, TT, 128])
        H2 = PT[:, 0:GROUPS].rearrange("p g t q -> p g (t q)")
        TN = sb("TN", [128, TOK])
        SQ = sb("SQ", [128, TOK])
        ATT = SQ
        V = sb("V", [128, TT, C])
        P = sb("P", [128, P_BUFFERS, TOK])
        HG = P
        UNUSED = sb("UNUSED", [128, 1])
        NEGMAX = sb("NEGMAX", [128, P_BUFFERS, 2])
        L = sb("L", [128, TT, HEADS_C])
        RX = TN[:, HALF:HALF + 2 * C].rearrange("p (b h c) -> p b h c", b=2, h=HEADS_C)
        RT = TN[:, HALF + 2 * C:HALF + 3 * C]
        ACC = PT[:, GROUPS]
        spare = PT[:, GROUPS + 1].rearrange("p t q -> p (t q)")
        PROBS, BEST, BEST_AT, COMB, PICK = (
            spare[:, i * TT * EXPERTS:(i + k) * TT * EXPERTS] for i, k in ((0, 1), (1, 1), (2, 1), (3, 1), (4, 2)))
        PROBS, BEST, BEST_AT, COMB = (v.rearrange("p (t e) -> p t e", t=TT) for v in (PROBS, BEST, BEST_AT, COMB))
        BEST_AT = BEST_AT.bitcast(U32)
        PICK = PICK.rearrange("p (k t e) -> p k t e", k=2, t=TT)
        RSTAT = spare[:, 6 * TT * EXPERTS:6 * TT * EXPERTS + 4 * TT].rearrange("p (i t) -> p i t", i=4)
        BEST_ATF, BEST_W = (spare[:, at:at + 2 * TT].rearrange("p (t k) -> p t k", t=TT)
                            for at in (7 * TT * EXPERTS, 8 * TT * EXPERTS))
        COMB_T = PT[0:EXPERTS, GROUPS - 1].rearrange("p t q -> p (t q)")

        psA = [ctx.enter_context(nc.psum_tensor(f"psA{i}", [128, HALF], F32)) for i in range(2)]
        psB = [ctx.enter_context(nc.psum_tensor(f"psB{i}", [128, 2 * HALF], F32)) for i in range(3)]

        weights_in = sem("weights_in")
        ready = sem("ready")
        x_in, raster_in, out_done = sem("x_in"), sem("raster_in"), sem("out_done")
        a_ready = [sem(f"a_ready{i}") for i in range(2)]
        a_free = [sem(f"a_free{i}") for i in range(2)]
        b_ready = [sem(f"b_ready{i}") for i in range(3)]
        b_free = [sem(f"b_free{i}") for i in range(3)]
        xsum_ready, kv_ready, table_in = sem("xsum_ready"), sem("kv_ready"), sem("table_in")
        v_ready, tap_ready, win_ready, chosen_ready = sem("v_ready"), sem("tap_ready"), sem("win_ready"), sem("chosen_ready")
        kvsel_in = [sem(f"kvsel_in{t}") for t in range(WTILES)]
        products_ready, products_summed = sem("products_ready"), sem("products_summed")
        s_ready, e_ready, attended_ready = sem("s_ready"), sem("e_ready"), sem("attended_ready")
        pv_done, lepe_done, x1_ready = sem("pv_done"), sem("lepe_done"), sem("x1_ready")
        h1_ready, h2_ready, x2_ready = sem("h1_ready"), sem("h2_ready"), sem("x2_ready")
        shifted_in = [sem(f"shifted_in{b}") for b in range(2)]
        centred_ready, square_ready, std_ready, rstd_ready, norm_ready = (
            sem("centred_ready"), sem("square_ready"), sem("std_ready"), sem("rstd_ready"), sem("norm_ready"))
        table_loaded = sem("table_loaded")
        high_ready, qk_ready, vt_ready = sem("high_ready"), sem("qk_ready"), sem("vt_ready")
        scaled_ready, p_ready = sem("scaled_ready"), sem("p_ready")
        rx_ready, att_ready = sem("rx_ready"), sem("att_ready")
        sum_ready, rsub_ready, rexp_ready = sem("sum_ready"), sem("rsub_ready"), sem("rexp_ready")
        comb_ready, combt_ready = sem("comb_ready"), sem("combt_ready")
        acc_ready, hg_ready, out_ready = sem("acc_ready"), sem("hg_ready"), sem("out_ready")
        fences = {e: sem(f"fence_{e}") for e in ("DVE", "Pool", "SP")}
        dve_a1, dve_a2, dve_b = sem("dve_a1"), sem("dve_a2"), sem("dve_b")
        dve_a2_image_0 = sem("dve_a2_image_0")

        table_rows = table.rearrange("(t p) f -> p t f", p=128)
        ident = w("ident")

        def products_before(m, t):
            return 2 * PX * (WTILES * (m - 1) + t)

        def fence(engine):
            engine.sem_inc(fences[engine.engine.name], 1)

        block = ctx.enter_context(nc.Block())

        @block.sync
        def _(sp):
            def load_x(m):
                sp.dma_start(X[:], x_by_window[bass.ds(m, 1)].rearrange("a c n -> (a c) n")).then_inc(x_in, 16)

            def load_raster(m):
                if not (isinstance(m, int) and m == 0):
                    sp.wait_ge(x1_ready, m)
                sp.dma_start(XLEPE[:], x[bass.ds(m, 1)].rearrange("a c n -> (a c) n")).then_inc(raster_in, 16)

            def x_is_free(m):
                for h in range(2):
                    sp.wait_ge(a_ready[RING_A.slot(("v", h))], RING_A.turn(("v", h), m - 1))
                sp.wait_ge(xsum_ready, m)

            def store_table(m):
                sp.wait_ge(kv_ready, m + 1)
                fence(sp)
                for t in range(WTILES):
                    if not (isinstance(m, int) and m == 0):
                        sp.wait_ge(kvsel_in[t], 16 * SLOTS * m)
                sp.dma_start(table_rows, KV[:].rearrange("p t x c -> p t (x c)")).then_inc(table_in, 16)

            def store_out(n):
                sp.wait_ge(out_ready, n + 1)
                sp.dma_start(out[bass.ds(n, 1)].rearrange("a (t p) c -> p (a t) c", p=128), ACC).then_inc(out_done, 16)

            def shift_h1(n, groups):
                for g in groups:
                    b = g % 2
                    sp.wait_ge(h1_ready, GROUPS * n + g + 1)
                    fence(sp)
                    if g >= 2:
                        before = ("dw", g - 2)
                        sp.wait_ge(b_ready[RING_B.slot(before)], RING_B.turn(before, n))
                    rows = H1_PAD[:, b].rearrange("c y x -> c (y x)")
                    for dx in range(3):
                        sp.dma_start(SHIFTED[32 * dx:32 * dx + 32, b, :, 0:PLANE - 2], rows[:, dx:dx + PLANE - 2]
                                     ).then_inc(shifted_in[b], 16)

            def image_traffic(n, second, first, after):
                shift_h1(n, (2, 3))
                if first is not None:
                    load_raster(first)
                    store_table(first)
                if second is not None:
                    shift_h1(second, (0, 1))
                store_out(n)
                if after is not None:
                    x_is_free(after)
                    load_x(after)

            sp.dma_start(W[:], packed).then_inc(weights_in, 16)
            sp.dma_start(PROD[:, 0:512 + DIAGONALS + 32], gains).then_inc(weights_in, 16)
            load_x(0)
            load_raster(0)
            store_table(0)
            x_is_free(1)
            load_x(1)
            load_raster(1)
            shift_h1(0, (0, 1))
            store_table(1)
            x_is_free(2)
            load_x(2)
            with sp.Fori(0, IMAGES - 3) as n:
                image_traffic(n, n + 1, n + 2, n + 3)
                fence(sp)
            image_traffic(IMAGES - 3, IMAGES - 2, IMAGES - 1, None)
            image_traffic(IMAGES - 2, IMAGES - 1, None, None)
            image_traffic(IMAGES - 1, None, None, None)
            sp.wait_ge(out_done, 16 * (IMAGES + 1))

        @block.tensor
        def _(pe):
            def two_halves(ps, lhs, rhs, **kw):
                for h in range(2):
                    mm = pe.matmul(ps[:, h * HALF:(h + 1) * HALF], lhs, rhs[:, h * HALF:(h + 1) * HALF], **kw)
                return mm

            whole = dict(start=True, stop=True)

            def open_a(name, m):
                s = RING_A.slot(name)
                pe.wait_ge(a_free[s], RING_A.turn(name, m))
                return psA[s], a_ready[s]

            def a_project(m, t, p):
                if t == 0 and p == 0:
                    pe.wait_ge(x_in, 16 * (m + 1))
                ps, done = open_a(("qkv", t, p), m)
                at = p * WINS + t * 128
                pe.matmul(ps[:, 0:384], X[:, at:at + 128], w("wqkv"), **whole).then_inc(done, 1)

            def a_values(m, h):
                ps, done = open_a(("v", h), m)
                pe.matmul(ps[:], w("wqkv", 256, 384), X[:, h * HALF:(h + 1) * HALF], **whole).then_inc(done, 1)

            def a_windows(m):
                pe.wait_ge(xsum_ready, m + 1)
                ps, done = open_a("windows", m)
                pe.matmul(ps[:, 0:WINS], w("wqkv", 0, 128), X_SUM4, **whole)
                pe.matmul(ps[:, WINS:2 * WINS], w("wqkv", 128, 256), X_SUM4, **whole).then_inc(done, 1)

            def a_logits(m):
                pe.wait_ge(win_ready, 2 * (m + 1))
                ps, done = open_a("logits", m)
                for t in range(WTILES):
                    mm = pe.matmul(ps[:, t * WINS:(t + 1) * WINS], QWIN[:, t * 128:(t + 1) * 128], KWIN, **whole)
                mm.then_inc(done, 1)

            def a_attended(m, t):
                pe.wait_ge(attended_ready, WTILES * m + t + 1)
                ps, done = open_a(("attended", t), m)
                for p in range(PX):
                    mm = pe.transpose(ps[:, p * 128:(p + 1) * 128], Q[:, t, p, :], ident)
                mm.then_inc(done, 1)

            def a_first_half(m):
                a_windows(m)
                a_logits(m)
                for t in range(WTILES):
                    for p in range(PX):
                        a_project(m, t, p)
                for h in range(2):
                    a_values(m, h)

            def emit(name, n):
                s = RING_B.slot(name)
                ps = psB[s]
                kind, i, half = (name + (0,))[:3] if isinstance(name, tuple) else (name, 0, 0)
                if kind == "fc1" and i == 0:
                    pe.wait_ge(x1_ready, n + 1)
                if kind == "dw":
                    pe.wait_ge(shifted_in[i % 2], 16 * 3 * (2 * n + i // 2 + 1))
                if kind == "fc2" and i == 0:
                    pe.wait_ge(h2_ready, GROUPS * (n + 1))
                if kind == "centred":
                    pe.wait_ge(x2_ready, 2 * (2 * n + i) + half + 1)
                if kind == "var":
                    pe.wait_ge(square_ready, 2 * (2 * n + i) + half + 1)
                if kind == "rstd":
                    pe.wait_ge(rstd_ready, 2 * (2 * n + i) + half + 1)
                if kind in ("v", "router"):
                    pe.wait_ge(norm_ready, 2 * (2 * n + (kind == "router") + 1))
                if kind == "scores" and i < HEADS_C:
                    pe.wait_ge(qk_ready, 2 * (HEADS_C * n + i + 1))
                if kind == "turned":
                    pe.wait_ge(p_ready, UNITS * n + i + 1)
                if kind == "wo":
                    pe.wait_ge(att_ready, TT * n + TT // 2 * (i + 1))
                if kind == "combine":
                    pe.wait_ge(comb_ready, n + 1)
                if kind == "start":
                    pe.wait_ge(sum_ready, 2 * (n + 1))
                if kind == "expert":
                    pe.wait_ge(hg_ready, EXPERTS * n + i + 1)
                pe.wait_ge(b_free[s], RING_B.turn(name, n))
                if kind == "fc1":
                    mm = two_halves(ps, w("fc1", 128 * i, 128 * i + 128), XR, **whole)
                elif kind == "dw":
                    for dy in range(3):
                        for h in range(2):
                            for q in range(4):
                                rows = SHIFTED[:, i % 2, q].rearrange("p (y x) -> p y x", y=MSIDE)[
                                    :, 16 * h + dy:16 * h + dy + 16, 0:SIDE]
                                mm = pe.matmul(ps[32 * q:32 * q + 32, h * HALF:(h + 1) * HALF],
                                               DIAG[:, 3 * (4 * i + q) + dy, :], rows, start=dy == 0, stop=dy == 2)
                elif kind == "fc2":
                    for g in range(GROUPS):
                        mm = pe.matmul(ps[:, 0:HALF], w("fc2", 128 * g, 128 * g + 128), H2[:, g, i * HALF:(i + 1) * HALF],
                                       start=g == 0, stop=g == GROUPS - 1)
                elif kind == "centred":
                    mm = pe.matmul(ps[:, 0:HALF], w("centring"), XR[:, half * HALF:(half + 1) * HALF], **whole)
                elif kind in ("var", "rstd"):
                    for t in range(TT // 2):
                        rows = SQ[:, half * HALF + t * 128:half * HALF + (t + 1) * 128]
                        if kind == "var":
                            mm = pe.matmul(ps[:, t:t + 1], rows, w("mean_w", 0, 1), **whole)
                        else:
                            mm = pe.transpose(ps[:, t * 128:(t + 1) * 128], rows, ident)
                elif kind in ("q", "k"):
                    mm = two_halves(ps[0:96], w("attn_" + kind, 96 * i, 96 * i + 96), TN, **whole)
                elif kind == "wo":
                    mm = pe.matmul(ps[:, 0:HALF], w("attn_vo", 128, 256), ATT[:, i * HALF:(i + 1) * HALF], **whole)
                elif kind == "v":
                    for t in range(TT):
                        mm = pe.matmul(ps[:, t * 128:(t + 1) * 128], TN[:, t * 128:(t + 1) * 128],
                                       w("attn_vo", 0, 128), **whole)
                elif kind == "scores":
                    q, h = divmod(i, HEADS_C)
                    mm = two_halves(ps, QS[0:96, h, q * 128:(q + 1) * 128].bitcast(F32R),
                                    KS[0:96, h].bitcast(F32R), **whole)
                elif kind == "turned":
                    for t in range(TT):
                        mm = pe.transpose(ps[:, t * 128:(t + 1) * 128], P[:, i % P_BUFFERS, t * 128:(t + 1) * 128], ident)
                elif kind == "router":
                    for t in range(TT):
                        mm = pe.matmul(ps[:, t * EXPERTS:(t + 1) * EXPERTS], TN[:, t * 128:(t + 1) * 128],
                                       w("router"), **whole)
                elif kind == "combine":
                    for t in range(TT):
                        mm = pe.transpose(ps[0:EXPERTS, t * 128:(t + 1) * 128], COMB[:, t, :], ident)
                elif kind == "start":
                    for t in range(TT):
                        cols = slice(t * 128, (t + 1) * 128)
                        pe.matmul(ps[:, cols], XR[:, cols], ident, start=t % (TT // 2) == 0, stop=False)
                    return
                elif kind == "hidden":
                    mm = two_halves(ps, w("w1", 128 * i, 128 * i + 128), TN, **whole)
                elif kind == "expert":
                    for t in range(TT):
                        mm = pe.matmul(ps[:, t * 128:(t + 1) * 128], HG[:, i % 2, t * 128:(t + 1) * 128],
                                       w("w2", 128 * i, 128 * i + 128), **whole)
                mm.then_inc(b_ready[s], 1)

            def start_completed(n):
                s = RING_B.slot("start")
                pe.wait_ge(combt_ready, n + 1)
                for t in range(TT):
                    cols = slice(t * 128, (t + 1) * 128)
                    mm = pe.matmul(psB[s][:, cols], COMB_T[:, cols], w("b2")[0:EXPERTS], start=False,
                                   stop=t % (TT // 2) == TT // 2 - 1)
                mm.then_inc(b_ready[s], 1)

            def times_values(c, part, n):
                s = RING_A.slot(("pv", c))
                if part == 0:
                    if c == 0:
                        pe.wait_ge(vt_ready, n + 1)
                    last = HEADS_C * (c + 1) - 1
                    for u in range(last + 1 - AHEAD, last + 1) if c == TT - 1 else [last]:
                        slot = RING_B.slot(("turned", u))
                        pe.wait_ge(b_free[slot], RING_B.turn(("turned", u), n) + 1)
                    pe.wait_ge(a_free[s], RING_A.turn(("pv", c), n))
                for t in range(part * TT // HEADS_C, (part + 1) * TT // HEADS_C):
                    for h in range(HEADS_C):
                        rows = slice(CH_C * h, CH_C * (h + 1))
                        pe.matmul(psA[s][rows, 0:128], V[:, t, rows], PT[:, (HEADS_C * c + h) % TURNED_BUFFERS, t, :],
                                  start=t == 0, stop=t == TT - 1)
                if part == HEADS_C - 1:
                    pe.wait_ge(rx_ready, TT * n + c + 1)
                    pe.transpose(psA[s][:, 128:256], RX[:, c % 2].rearrange("p h c -> p (h c)"), ident
                                 ).then_inc(a_ready[s], 1)

            def behind(u, n):
                c, part = divmod(u, HEADS_C)
                if c > 0:
                    times_values(c - 1, part, n)

            def stages_b_to_d(n, second, first):
                for name in ORDER_B:
                    if name not in RING_B.early:
                        emit(name, n)
                    elif second is not None:
                        emit(name, second)
                    if name[0] == "scores" and name[1] >= AHEAD:
                        behind(name[1] - AHEAD, n)
                    if name[0] == "turned" and name[1] + AHEAD >= UNITS:
                        behind(name[1], n)
                    if name == ("turned", UNITS - 1):
                        for part in range(HEADS_C):
                            times_values(TT - 1, part, n)
                    if second is not None and name in (("var", 1, 0), ("wo", 1)):
                        a_attended(second, int(name[0] == "wo"))
                    if first is not None:
                        for t, p in PROJECTIONS_AFTER.get(name, []):
                            a_project(first, t, p)
                        if name == ("centred", 1, 1):
                            a_windows(first)
                        if name == ("var", 1, 1):
                            a_logits(first)
                        if name == ("hidden", 3):
                            for h in range(2):
                                a_values(first, h)
                    if name == ("hidden", 1):
                        start_completed(n)
                        if first is not None:
                            for t, p in PROJECTIONS_AFTER["start completed"]:
                                a_project(first, t, p)

            pe.wait_ge(weights_in, 32)
            pe.wait_ge(ready, 3)
            a_first_half(0)
            for t in range(WTILES):
                a_attended(0, t)
            for name in RING_B.early:
                emit(name, 0)
            a_first_half(1)
            with pe.Fori(0, IMAGES - 2) as n:
                stages_b_to_d(n, n + 1, n + 2)
            stages_b_to_d(IMAGES - 2, IMAGES - 1, None)
            stages_b_to_d(IMAGES - 1, None, None)

        @block.scalar
        def _(act):
            def a_values(m):
                if not (isinstance(m, int) and m == 0):
                    act.wait_ge(lepe_done, TAPS5 * m)
                for hy in range(2):
                    s = RING_A.slot(("v", hy))
                    act.wait_ge(a_ready[s], RING_A.turn(("v", hy), m))
                    for wx in range(2):
                        act.activation(V_PAD[:, 2 + hy:2 + hy + SIDE:2, 2 + wx:2 + wx + SIDE:2],
                                       psA[s][:, wx * WINS:(wx + 1) * WINS].rearrange("c (j i) -> c j i", i=WIN_SIDE),
                                       ACT.Identity, bias=col("bv_a")).then_inc(v_ready, 1)
                    act.wait_ge(v_ready, PX * m + 2 * hy + 2)
                    act.sem_inc(a_free[s], 1)

            def a_windows(m):
                s = RING_A.slot("windows")
                act.wait_ge(a_ready[s], RING_A.turn("windows", m))
                for i, (out, bias) in enumerate(((QWIN, "bq_a"), (KWIN, "bk_a"))):
                    act.activation(out, psA[s][:, i * WINS:(i + 1) * WINS], ACT.Identity, bias=col(bias),
                                   scale=1.0 / PX).then_inc(win_ready, 1)
                act.wait_ge(win_ready, 2 * (m + 1))
                act.sem_inc(a_free[s], 1)

            def a_exp(t, m):
                act.wait_ge(s_ready, WTILES * m + t + 1)
                act.activation(S[t], S[t], ACT.Exp, scale=SCALE_A).then_inc(e_ready, 1)

            def evacuate(name, n, signal, *ops):
                s = RING_B.slot(name)
                act.wait_ge(b_ready[s], RING_B.turn(name, n))
                for op in ops[:-1]:
                    op(psB[s])
                ops[-1](psB[s]).then_inc(b_free[s], 1)
                act.wait_ge(b_free[s], RING_B.turn(name, n) + 1)
                act.sem_inc(signal, 1)

            def fc1(g, n):
                if g >= 2:
                    act.wait_ge(shifted_in[g % 2], 16 * 3 * (2 * n + 1))
                evacuate(("fc1", g), n, h1_ready, lambda ps: act.activation(
                    H1_PAD[:, g % 2, 1:1 + SIDE, 1:1 + SIDE], ps[:].rearrange("c (y x) -> c y x", y=SIDE),
                    ACT.Identity, bias=col("b_fc1", g), scale=col("g_fc1", g)))

            def dw(g, n):
                evacuate(("dw", g), n, h2_ready, lambda ps: act.activation(
                    H2[:, g, :], ps[:], ACT.Relu, bias=col("b_dw", g)))

            def centred(i, half, n):
                s = RING_B.slot(("centred", i, half))
                turn = RING_B.turn(("centred", i, half), n)
                act.wait_ge(b_ready[s], turn)
                cols = slice(half * HALF, (half + 1) * HALF)
                act.activation(SQ[:, cols], psB[s][:, 0:HALF], ACT.Square).then_inc(square_ready, 1)
                act.activation(TN[:, cols], psB[s][:, 0:HALF], ACT.Copy).then_inc(b_free[s], 1)
                act.wait_ge(square_ready, 2 * (2 * n + i) + half + 1)
                act.wait_ge(b_free[s], turn + 1)
                act.sem_inc(centred_ready, 1)

            def deviation(i, half, n):
                evacuate(("var", i, half), n, std_ready, lambda ps: act.activation(
                    STD[:, half], ps[:, 0:TT // 2], ACT.Sqrt, bias=col("eps")))

            def load_table(function, turn, n):
                act.wait_ge(table_loaded, TABLES * n + turn + 1)
                act.activation(UNUSED[:], w("mean_w", 0, 1), function).then_inc(table_loaded, 1)

            def exp(u, n):
                act.wait_ge(scaled_ready, UNITS * n + u + 1)
                q, h = divmod(u, HEADS_C)
                b = u % P_BUFFERS
                act.activation(P[:, b, :], P[:, b, :], ACT.Exp, bias=NEGMAX[:, b, 1:2],
                               accum_out=L[:, q, h:h + 1]).then_inc(p_ready, 1)

            def turned(u, n):
                if u == GROUPS:
                    act.wait_ge(out_done, 16 * (n + 1))
                s = RING_B.slot(("turned", u))
                act.wait_ge(b_ready[s], RING_B.turn(("turned", u), n))
                act.activation(PT[:, u % TURNED_BUFFERS].rearrange("k t q -> k (t q)"), psB[s][:], ACT.Copy
                               ).then_inc(b_free[s], 1)

            def stages_b_to_d(n, second, first):
                fc1(2, n)
                dw(0, n)
                if second is not None:
                    a_exp(0, second)
                fc1(3, n)
                dw(1, n)
                dw(2, n)
                dw(3, n)
                load_table(ACT.Sqrt, 0, n)
                for half in range(2):
                    centred(0, half, n)
                for half in range(2):
                    deviation(0, half, n)
                load_table(ACT.Exp, 1, n)
                for h in range(HEADS_C):
                    if h == 3:
                        exp(0, n)
                    for kind, stacked in (("q", QS), ("k", KS)):
                        if h == 3 and kind == "k":
                            turned(0, n)
                        s = RING_B.slot((kind, h))
                        act.wait_ge(b_ready[s], RING_B.turn((kind, h), n))
                        act.activation(stacked[0:96, h].bitcast(F32R), psB[s][0:96, :], ACT.Identity,
                                       bias=col(f"b{kind}_c", h)[0:96]).then_inc(high_ready, 1)
                exp(1, n)
                for u in range(1, UNITS):
                    if u + 1 < UNITS:
                        exp(u + 1, n)
                    turned(u, n)
                    if second is not None and u == WINDOW_STEPS_AT[STEPS_TO_SOFTMAX - EARLY_STEPS - MLP_STEPS] - 1:
                        a_exp(1, second)
                    if u == PROJECTED + 3:
                        centred(1, 0, n)
                load_table(ACT.Sqrt, 2, n)
                deviation(1, 0, n)
                if first is not None:
                    a_windows(first)
                centred(1, 1, n)
                deviation(1, 1, n)
                load_table(ACT.Exp, 3, n)
                act.wait_ge(rsub_ready, n + 1)
                act.activation(PROBS, PROBS, ACT.Exp).then_inc(rexp_ready, 1)
                load_table(ACT.Gelu, 4, n)

                def gelu(e):
                    evacuate(("hidden", e), n, hg_ready, lambda ps: act.activation(
                        HG[:, e % 2, :], ps[:], ACT.Gelu, bias=col("b1", e)))

                gelu(0)
                evacuate("combine", n, combt_ready, lambda ps: act.activation(COMB_T[:], ps[0:EXPERTS, :], ACT.Copy))
                gelu(1)
                evacuate("start", n, acc_ready, lambda ps: act.activation(
                    ACC.rearrange("p t c -> p (t c)"), ps[:], ACT.Copy))
                for e in range(2, EXPERTS):
                    gelu(e)
                    if first is not None and e == 3:
                        a_values(first)
                    if second is not None and e - 2 in (NEXT_IMAGE, NEXT_IMAGE + 1):
                        fc1(e - 2 - NEXT_IMAGE, second)
                load_table(ACT.Exp, 5, n)

            act.wait_ge(weights_in, 32)
            act.wait_ge(ready, 3)
            a_windows(0)
            a_values(0)
            a_exp(0, 0)
            a_exp(1, 0)
            fc1(0, 0)
            fc1(1, 0)
            a_windows(1)
            a_values(1)
            with act.Fori(0, IMAGES - 2) as n:
                stages_b_to_d(n, n + 1, n + 2)
            stages_b_to_d(IMAGES - 2, IMAGES - 1, None)
            stages_b_to_d(IMAGES - 1, None, None)

        @block.vector
        def _(dve):
            class Chain:

                def __init__(self, counter, per_image):
                    self.counter, self.per_image = counter, per_image

                def at_image(self, n, done=0):
                    self.base, self.k = n * self.per_image, done

                def mark(self, ins):
                    self.k += 1
                    ins.then_inc(self.counter, 1)

                def settle(self):
                    if self.k:
                        dve.wait_ge(self.counter, self.base + self.k)

                def link(self, ins):
                    self.mark(ins)
                    self.settle()

                def check(self):
                    assert self.k == self.per_image, (self.counter, self.k)

            first_chain, chain_b = Chain(dve_a1, LINKS_A1), Chain(dve_b, LINKS_B)
            image_0_chain, later_chain = Chain(dve_a2_image_0, LINKS_A2 + 2 * WTILES * PX), Chain(dve_a2, LINKS_A2)

            def second_chain(m):
                return image_0_chain if isinstance(m, int) and m == 0 else later_chain

            def first_half(m):
                chain = first_chain

                def sums():
                    chain.at_image(m)
                    dve.wait_ge(x_in, 16 * (m + 1))
                    dve.tensor_reduce(X_SUM4, X[:].rearrange("c (p w) -> c w p", p=PX), AX.X,
                                      ALU.add).then_inc(xsum_ready, 1)

                def rows(t, p):
                    if t == 0 and p == 0 and not (isinstance(m, int) and m == 0):
                        dve.wait_ge(table_in, 16 * m)
                        dve.wait_ge(lepe_done, TAPS5 * m)
                    s = RING_A.slot(("qkv", t, p))
                    dve.wait_ge(a_ready[s], RING_A.turn(("qkv", t, p), m))
                    bias = w("qkv_bias")
                    chain.mark(dve.tensor_tensor(Q[:, t, p, :], psA[s][:, 0:128], bias[:, 0:128], ALU.add))
                    chain.mark(dve.tensor_tensor(KV[:, t, p, :], psA[s][:, 128:384], bias[:, 128:384], ALU.add))
                    chain.settle()
                    dve.sem_inc(a_free[s], 1)
                    if t == WTILES - 1 and p == PX - 1:
                        dve.sem_inc(kv_ready, 1)
                        chain.check()

                def choose():
                    s = RING_A.slot("logits")
                    dve.wait_ge(a_ready[s], RING_A.turn("logits", m))
                    fence(dve)
                    for t in range(WTILES):
                        chain.mark(dve.max(TOP[:, t, :], psA[s][:, t * WINS:(t + 1) * WINS]))
                    chain.settle()
                    fence(dve)
                    for t in range(WTILES):
                        chain.mark(dve.max_index(CHOSEN[:, t, :], TOP[:, t, :], psA[s][:, t * WINS:(t + 1) * WINS]))
                    chain.settle()
                    dve.sem_inc(a_free[s], 1)
                    dve.sem_inc(chosen_ready, 1)

                return [sums, choose] + [lambda t=t, p=p: rows(t, p) for t in range(WTILES) for p in range(PX)]

            def second_half(m):
                chain = second_chain(m)
                alone = isinstance(m, int) and m == 0

                def multiply_keys(t, q):
                    if q == 0:
                        dve.wait_ge(kvsel_in[t], 16 * SLOTS * (m + 1))
                    chain.settle()
                    chain.mark(dve.tensor_tensor(PROD[:].rearrange("p (k c) -> p k c", k=KEYS), KVSEL[:, t, :, 0:C],
                                                 Q[:, t, q, :].unsqueeze(1).broadcast_to([128, KEYS, C]), ALU.mult))

                def sum_channels(t, q):
                    chain.settle()
                    chain.mark(dve.tensor_reduce(S[t][:, q], PROD[:].rearrange("p (k h c) -> p k h c", k=KEYS, c=CH_A),
                                                 AX.X, ALU.add))

                def sum_products(t, i):
                    dve.wait_ge(products_ready, products_before(m, t) + i + 1)
                    q, half = divmod(i, 2)
                    keys = slice(half * KEYS // 2, (half + 1) * KEYS // 2)
                    dve.tensor_reduce(S[t][:, q, keys, :], PRODUCTS[i % 2].rearrange("p (k h c) -> p k h c", h=HEADS_A, c=CH_A),
                                      AX.X, ALU.add).then_inc(products_summed, 1)

                def less_maximum(t):
                    top, by_head = SUMS[:, 0, :], S[t].rearrange("p q k h -> p q h k")
                    chain.settle()
                    if not alone:
                        dve.wait_ge(products_summed, products_before(m, t) + 2 * PX)
                        if t == 1:
                            dve.wait_ge(kvsel_in[t], 16 * SLOTS * (m + 1))
                    chain.link(dve.tensor_reduce(top.rearrange("p (q h) -> p q h", q=PX), by_head, AX.X, ALU.max))
                    dve.tensor_tensor(S[t], S[t], top.rearrange("p (q h) -> p q h", q=PX).unsqueeze(2)
                                      .broadcast_to([128, PX, KEYS, HEADS_A]), ALU.subtract).then_inc(s_ready, 1)

                def sum_keys(t):
                    dve.wait_ge(e_ready, WTILES * m + t + 1)
                    chain.link(dve.tensor_reduce(SUMS[:, 0, :].rearrange("p (q h) -> p q h", q=PX),
                                                 S[t].rearrange("p q k h -> p q h k"), AX.X, ALU.add))
                    chain.mark(dve.reciprocal(SUMS[:, 1, :], SUMS[:, 0, :]))

                def multiply_values(t, q):
                    if not alone and q == 0:
                        dve.wait_ge(kvsel_in[t], 16 * SLOTS * (m + 1))
                    chain.settle()
                    chain.mark(dve.tensor_tensor(PROD[:].rearrange("p (k h c) -> p k h c", k=KEYS, h=HEADS_A),
                                                 KVSEL[:, t, :, C:2 * C].rearrange("p k (h c) -> p k h c", h=HEADS_A),
                                                 S[t][:, q].unsqueeze(3).broadcast_to([128, KEYS, HEADS_A, CH_A]),
                                                 ALU.mult))

                def attend(t, q):
                    chain.settle()
                    chain.mark(dve.tensor_reduce(Q[:, t, q, :], PROD[:].rearrange("p (k f) -> p f k", k=KEYS),
                                                 AX.X, ALU.add))
                    if q == PX - 1:
                        chain.settle()
                        dve.sem_inc(pv_done, 1)
                        heads = Q[:, t].rearrange("p q (h c) -> p (q h) c", h=HEADS_A)
                        dve.tensor_tensor(heads, heads, SUMS[:, 1, :].unsqueeze(2)
                                          .broadcast_to([128, PX * HEADS_A, CH_A]), ALU.mult).then_inc(attended_ready, 1)

                def key_steps(t):
                    if not alone:
                        return [lambda t=t, i=i: sum_products(t, i) for i in range(2 * PX)]
                    return [step for q in range(PX)
                            for step in (lambda t=t, q=q: multiply_keys(t, q), lambda t=t, q=q: sum_channels(t, q))]

                def softmax_steps(t):
                    return [lambda: less_maximum(t), lambda: sum_keys(t)]

                def value_steps(t):
                    return [step for q in range(PX)
                            for step in (lambda t=t, q=q: multiply_values(t, q), lambda t=t, q=q: attend(t, q))]

                if alone:
                    return [step for t in range(WTILES) for step in key_steps(t) + softmax_steps(t) + value_steps(t)]
                woven = [step for pair in zip(value_steps(0), key_steps(1)) for step in pair]
                return key_steps(0) + softmax_steps(0) + woven + softmax_steps(1) + value_steps(1)

            def window_residual(m, t):
                if t == 0:
                    dve.wait_ge(lepe_done, TAPS5 * (m + 1))
                dims = dict(j=WIN_SIDE, hy=2, i=WIN_SIDE, wx=2)
                s = RING_A.slot(("attended", t))
                dve.wait_ge(a_ready[s], RING_A.turn(("attended", t), m))
                for p in range(PX):
                    hy, wx = divmod(p, 2)
                    place = XLEPE[:].rearrange("c (j hy i wx) -> c hy j i wx", **dims)[:, hy, 8 * t:8 * t + 8, :, wx]
                    second_chain(m).mark(dve.scalar_tensor_tensor(
                        out=place, in0=psA[s][:, p * 128:(p + 1) * 128].rearrange("c (j i) -> c j i", j=8),
                        scalar=col("b_lepe"), in1=place, op0=ALU.add, op1=ALU.add))
                second_chain(m).settle()
                dve.sem_inc(a_free[s], 1)

            def to_stream(m):
                if not (isinstance(m, int) and m == 0):
                    s = RING_B.slot("start")
                    dve.wait_ge(b_ready[s], RING_B.turn("start", m - 1))
                dve.tensor_copy(XR[:], XLEPE[:]).then_inc(x1_ready, 1)
                second_chain(m).check()

            def stages_b_to_d(n, second, first):
                link = chain_b.link
                chain_b.at_image(n)
                steps = []
                if second is not None:
                    later_chain.at_image(second - 1)
                    steps = second_half(second)[EARLY_STEPS:]
                later = second_half(first)[:EARLY_STEPS] if first is not None else []
                front = first_half(first) if first is not None else []

                def run(queue, count):
                    for _ in range(min(count, len(queue))):
                        queue.pop(0)()

                def arrived(name):
                    s = RING_B.slot(name)
                    dve.wait_ge(b_ready[s], RING_B.turn(name, n))
                    return psB[s], b_free[s]

                def columns(half):
                    return slice(half * HALF, (half + 1) * HALF)

                def residual_add(name, half, bias):
                    ps, free = arrived((name, half))
                    x = XR[:, columns(half)]
                    link(dve.scalar_tensor_tensor(out=x, in0=ps[:, 0:HALF], scalar=bias, in1=x, op0=ALU.add, op1=ALU.add))
                    dve.sem_inc(free, 1)
                    dve.sem_inc(x2_ready, 1)

                def spread(i, half):
                    dve.wait_ge(std_ready, 2 * (2 * n + i) + half + 1)
                    link(dve.reciprocal(STD[:, half], STD[:, half]))
                    dve.tensor_copy(SQ[:, columns(half)].rearrange("p (t c) -> p t c", c=C), STD[:, half].unsqueeze(2)
                                    .broadcast_to([128, TT // 2, C])).then_inc(rstd_ready, 1)

                def normalise(i, half):
                    ps, free = arrived(("rstd", i, half))
                    dve.wait_ge(centred_ready, 2 * (2 * n + i) + half + 1)
                    link(dve.tensor_tensor(TN[:, columns(half)], TN[:, columns(half)], ps[:, 0:HALF], ALU.mult))
                    dve.sem_inc(free, 1)
                    dve.sem_inc(norm_ready, 1)

                def scale_scores(u):
                    ps, free = arrived(("scores", u))
                    b = u % P_BUFFERS
                    at = TOK - 128 - 128 * (u // HEADS_C)
                    fence(dve)
                    dve.tensor_tensor_reduce(P[:, b, :], ps[:], w("band", at, at + TOK), 1.0, -3.0e38,
                                             ALU.mult, ALU.max, NEGMAX[:, b, 0:1]).then_inc(free, 1)
                    negate_maximum(u)

                def negate_maximum(u):
                    s, b = RING_B.slot(("scores", u)), u % P_BUFFERS
                    dve.wait_ge(b_free[s], RING_B.turn(("scores", u), n) + 1)
                    dve.tensor_scalar(NEGMAX[:, b, 1:2], NEGMAX[:, b, 0:1], -1.0, None,
                                      ALU.mult).then_inc(scaled_ready, 1)

                def normaliser(c):
                    dve.wait_ge(p_ready, UNITS * n + HEADS_C * (c + 1))
                    link(dve.reciprocal(L[:, c, :], L[:, c, :]))
                    dve.tensor_copy(RX[:, c % 2], L[:, c, :].unsqueeze(2).broadcast_to([128, HEADS_C, CH_C])
                                    ).then_inc(rx_ready, 1)

                def attended(c):
                    s = RING_A.slot(("pv", c))
                    dve.wait_ge(a_ready[s], RING_A.turn(("pv", c), n))
                    link(dve.tensor_copy(RT, psA[s][:, 128:256]))
                    link(dve.tensor_tensor(ATT[:, 128 * c:128 * (c + 1)], psA[s][:, 0:128], RT, ALU.mult))
                    dve.sem_inc(a_free[s], 1)
                    dve.sem_inc(att_ready, 1)

                run(steps, MLP_STEPS)
                for half in range(2):
                    residual_add("fc2", half, col("b_fc2"))
                for half in range(2):
                    spread(0, half)
                for half in range(2):
                    normalise(0, half)
                ps, free = arrived("v")
                link(dve.tensor_tensor(V[:], ps[:].rearrange("p (t c) -> p t c", t=TT),
                                       w("bv_row").unsqueeze(1).broadcast_to([128, TT, C]), ALU.add))
                dve.sem_inc(free, 1)
                dve.sem_inc(vt_ready, 1)
                for h in range(HEADS_C):
                    for j, (kind, stacked, rows) in enumerate((("q", QS, slice(64, 96)), ("k", KS, slice(32, 64)))):
                        ps, free = arrived((kind, h))
                        dve.wait_ge(high_ready, 2 * (HEADS_C * n + h) + j + 1)
                        link(dve.scalar_tensor_tensor(out=stacked[rows, h].bitcast(F32R), in0=ps[rows, :],
                                                      scalar=col(f"b{kind}_c", h)[rows], in1=stacked[rows, h],
                                                      op0=ALU.add, op1=ALU.subtract))
                        dve.sem_inc(free, 1)
                        dve.sem_inc(qk_ready, 1)
                    if h > 0:
                        scale_scores(h - 1)
                for u in range(HEADS_C - 1, UNITS):
                    scale_scores(u)
                    if u in WINDOW_STEPS_AT:
                        run(steps, 1)
                    if u % HEADS_C == 2 and u >= HEADS_C:
                        normaliser(u // HEADS_C - 1)
                    if u % HEADS_C == HEADS_C - 1 and u >= 2 * HEADS_C:
                        attended(u // HEADS_C - 2)
                    if u == PROJECTED + 3:
                        residual_add("wo", 0, col("bo_c"))
                run(steps, 16)
                normaliser(TT - 1)
                assert not steps
                run(front, 1)
                attended(TT - 2)
                attended(TT - 1)
                spread(1, 0)
                residual_add("wo", 1, col("bo_c"))
                if second is not None:
                    window_residual(second, 0)
                normalise(1, 0)
                if second is not None:
                    window_residual(second, 1)
                spread(1, 1)
                dve.tensor_tensor(XR[:, columns(0)], XR[:, columns(0)], TN[:, columns(0)], ALU.add).then_inc(sum_ready, 1)
                normalise(1, 1)
                dve.tensor_tensor(XR[:, columns(1)], XR[:, columns(1)], TN[:, columns(1)], ALU.add).then_inc(sum_ready, 1)
                ps, free = arrived("router")
                logits = ps[:, 0:TT * EXPERTS].rearrange("p (t e) -> p t e", t=TT)
                over_e = [128, TT, EXPERTS]
                link(dve.tensor_reduce(RSTAT[:, 0, :], logits, AX.X, ALU.max))
                link(dve.tensor_tensor(PROBS, logits, RSTAT[:, 0, :].unsqueeze(2).broadcast_to(over_e), ALU.subtract))
                dve.sem_inc(free, 1)
                dve.sem_inc(rsub_ready, 1)
                dve.wait_ge(rexp_ready, n + 1)
                link(dve.tensor_reduce(RSTAT[:, 1, :], PROBS, AX.X, ALU.add))
                link(dve.reciprocal(RSTAT[:, 2, :], RSTAT[:, 1, :]))
                link(dve.tensor_tensor(PROBS, PROBS, RSTAT[:, 2, :].unsqueeze(2).broadcast_to(over_e), ALU.mult))
                fence(dve)
                for t in range(TT):
                    last = dve.max(BEST[:, t, :], PROBS[:, t, :])
                link(last)
                fence(dve)
                for t in range(TT):
                    last = dve.max_index(BEST_AT[:, t, :], BEST[:, t, :], PROBS[:, t, :])
                link(last)
                link(dve.tensor_tensor(RSTAT[:, 0, :], BEST[:, :, 0], BEST[:, :, 1], ALU.add))
                link(dve.tensor_scalar(RSTAT[:, 1, :], RSTAT[:, 0, :], 1e-12, None, ALU.max))
                link(dve.reciprocal(RSTAT[:, 2, :], RSTAT[:, 1, :]))
                dve.tensor_tensor(BEST_W, BEST[:, :, 0:2], RSTAT[:, 2, :].unsqueeze(2).broadcast_to([128, TT, 2]), ALU.mult)
                link(dve.tensor_copy(BEST_ATF, BEST_AT[:, :, 0:2]))
                iota = w("iota").rearrange("p (t e) -> p t e", t=TT)
                for k in range(2):
                    last = dve.tensor_tensor(PICK[:, k], iota, BEST_ATF[:, :, k:k + 1].broadcast_to(over_e), ALU.is_equal)
                link(last)
                for k in range(2):
                    last = dve.tensor_tensor(PICK[:, k], PICK[:, k], BEST_W[:, :, k:k + 1].broadcast_to(over_e), ALU.mult)
                link(last)
                link(dve.tensor_tensor(COMB, PICK[:, 0], PICK[:, 1], ALU.add))
                dve.sem_inc(comb_ready, 1)
                run(front, 8)
                dve.wait_ge(acc_ready, n + 1)
                for e in range(EXPERTS):
                    ps, free = arrived(("expert", e))
                    for t in range(TT):
                        last = dve.scalar_tensor_tensor(out=ACC[:, t, :], in0=ps[:, t * 128:(t + 1) * 128],
                                                        scalar=COMB[:, t, e:e + 1], in1=ACC[:, t, :],
                                                        op0=ALU.mult, op1=ALU.add)
                    link(last)
                    dve.sem_inc(free, 1)
                    if e == 0 and second is not None:
                        to_stream(second)
                    run(front, {0: 1}.get(e, 0))
                    run(later, {4: 1, 5: 1, 6: 2, 7: 2}.get(e, 0))
                dve.sem_inc(out_ready, 1)
                chain_b.check()

            dve.wait_ge(weights_in, 32)
            dve.tensor_tensor(w("wqkv"), w("wqkv"), PROD[:, 0:384], ALU.mult)
            for g in range(GROUPS):
                wg = w("fc2", 128 * g, 128 * g + 128)
                dve.tensor_tensor(wg, wg, PROD[:, 384:512], ALU.mult)
            shape = [128, DIAGONALS, 32]
            taps, eye = PROD[:, 512:512 + DIAGONALS], PROD[:, 512 + DIAGONALS:512 + DIAGONALS + 32]
            dve.tensor_tensor(DIAG[:], eye.unsqueeze(1).broadcast_to(shape), taps.unsqueeze(2).broadcast_to(shape),
                              ALU.mult).then_inc(ready, 1)
            dve.wait_ge(ready, 3)
            image_0_chain.at_image(0)
            for step in first_half(0) + second_half(0):
                step()
            for t in range(WTILES):
                window_residual(0, t)
            to_stream(0)
            for step in first_half(1) + second_half(1)[:EARLY_STEPS]:
                step()
            with dve.Fori(0, IMAGES - 2) as n:
                stages_b_to_d(n, n + 1, n + 2)
            stages_b_to_d(IMAGES - 2, IMAGES - 1, None)
            stages_b_to_d(IMAGES - 1, None, None)

        @block.gpsimd
        def _(pool):
            def gathers(m, t):
                if t == 0:
                    pool.wait_ge(chosen_ready, m + 1)
                    pool.wait_ge(table_in, 16 * (m + 1))
                    if not (isinstance(m, int) and m == 0):
                        pool.wait_ge(pv_done, WTILES * m)
                    fence(pool)
                for s in range(SLOTS):
                    pool.indirect_dma_start(
                        KVSEL[:, t, PX * s:PX * (s + 1), :].rearrange("p x c -> p (x c)"), None, table,
                        bass.IndirectOffsetOnAxis(ap=CHOSEN[:, t, s:s + 1], axis=0)).then_inc(kvsel_in[t], 16)

            def key_product(m, t, i):
                if i == 0:
                    pool.wait_ge(kvsel_in[t], 16 * SLOTS * (m + 1))
                if t == 1 or i > 1:
                    pool.wait_ge(products_summed, products_before(m, t) + i - 1)
                q, half = divmod(i, 2)
                keys = slice(half * KEYS // 2, (half + 1) * KEYS // 2)
                pool.tensor_tensor(PRODUCTS[i % 2].rearrange("p (k c) -> p k c", c=C), KVSEL[:, t, keys, 0:C],
                                   Q[:, t, q, :].unsqueeze(1).broadcast_to([128, KEYS // 2, C]), ALU.mult
                                   ).then_inc(products_ready, 1)

            def taps(m):
                pool.wait_ge(raster_in, 16 * (m + 1))
                pool.wait_ge(v_ready, PX * (m + 1))
                acc = XLEPE[:].rearrange("c (y x) -> c y x", y=SIDE)
                product = TAP.rearrange("c (y x) -> c y x", y=SIDE)
                for tap in range(TAPS5):
                    dy, dx = divmod(tap, 5)
                    fence(pool)
                    pool.tensor_scalar(product, V_PAD[:, dy:dy + SIDE, dx:dx + SIDE], col("lepe_w", tap), 0.0,
                                       ALU.mult, ALU.add).then_inc(tap_ready, 1)
                    pool.wait_ge(tap_ready, TAPS5 * m + tap + 1)
                    pool.tensor_tensor(acc, acc, product, ALU.add).then_inc(lepe_done, 1)
                    pool.wait_ge(lepe_done, TAPS5 * m + tap + 1)

            pool.memset(V_PAD[:], 0.0).then_inc(ready, 1)
            pool.memset(H1_PAD[:], 0.0)
            pool.memset(STACKED[:], 0.0).then_inc(ready, 1)
            for s in range(2):
                pool.sem_inc(a_free[s], 1)
            for s in range(3):
                pool.sem_inc(b_free[s], 1)
            pool.sem_inc(out_done, 16)
            pool.sem_inc(table_loaded, 1)
            pool.wait_ge(weights_in, 32)

            def window_stage(m):
                gathers(m, 0)
                for i in range(2 * PX):
                    if i == 2:
                        gathers(m, 1)
                    key_product(m, 0, i)
                for i in range(2 * PX):
                    key_product(m, 1, i)
                pool.wait_ge(products_summed, products_before(m, WTILES))
                taps(m)

            for t in range(WTILES):
                gathers(0, t)
            taps(0)
            window_stage(1)
            with pool.Fori(0, IMAGES - 2) as n:
                window_stage(n + 2)


def kernel(**inputs):
    import numpy as np
    import concourse.bacc as bacc
    from concourse.bass_utils import run_bass_kernel_spmd

    a = {k: np.asarray(v) for k, v in inputs.items()}
    f32 = np.float32

    def cols(v):
        return v.reshape(-1, 128).T

    def everywhere(v):
        return np.broadcast_to(v.reshape(1, -1), (128, v.size))

    L0 = {k[8:]: v for k, v in a.items() if k.startswith("L0_conv_")}
    L1 = {k[3:]: v for k, v in a.items() if k.startswith("L1_")}
    def thrice(m):
        rows = m.shape[0]
        return np.broadcast_to(m.reshape(rows, HEADS_C, 1, CH_C), (rows, HEADS_C, 3, CH_C)).reshape(rows, -1)

    def by_quarter(m):
        return m.transpose(0, 2, 1, 3).reshape(GROUPS, 128, -1)

    dw = np.zeros((128, DIAGONALS), f32)
    dw[:96] = L0["w_dw"].reshape(GROUPS, 32, 4, 3, 3).transpose(4, 1, 0, 2, 3).reshape(96, -1)
    eye = np.zeros((128, 32), f32)
    eye[:96] = np.tile(np.eye(32, dtype=f32), (3, 1))
    b2 = np.zeros((128, 128), f32)
    b2[:EXPERTS] = L1["ffn_b2"]
    distance = np.abs(np.arange(BAND)[None, :] - (TOK - 128) - np.arange(128)[:, None])
    band = ((TOK - distance) / TOK / np.sqrt(CH_C)).astype(f32)
    parts = {
        "wqkv": np.concatenate([L0["wq"].T, L0["wkv"].T], 1),
        "qkv_bias": everywhere(np.concatenate([L0["bq"], L0["bkv"]])),
        "fc1": L0["w_fc1"].T,
        "fc2": by_quarter(L0["w_fc2"].T.reshape(GROUPS, 32, 4, 128)).transpose(1, 0, 2).reshape(128, -1),
        "attn_q": thrice(L1["attn_Wq"]), "attn_k": thrice(L1["attn_Wk"]),
        "attn_vo": np.concatenate([L1["attn_Wv"], L1["attn_Wo"]], 1),
        "bv_row": everywhere(L1["attn_bv"]),
        "router": L1["ffn_router_w"].T,
        "w1": L1["ffn_w1"].transpose(1, 0, 2).reshape(128, -1),
        "w2": L1["ffn_w2"].transpose(1, 0, 2).reshape(128, -1),
        "b2": b2,
        "lepe_w": L0["w_lepe"].reshape(128, TAPS5),
        "bq_a": cols(L0["bq"]), "bk_a": cols(L0["bkv"][:128]), "bv_a": cols(L0["bkv"][128:]),
        "b_lepe": cols(L0["b_lepe"]), "g_fc1": cols(L0["g_fc1"]), "b_fc1": cols(L0["b_fc1"]),
        "b_dw": by_quarter(L0["b_dw"].reshape(GROUPS, 32, 4, 1))[:, :, 0].T, "b_fc2": cols(L0["b_fc2"]),
        "bq_c": thrice(L1["attn_bq"][None]).reshape(HEADS_C, 96).T, "bk_c": thrice(L1["attn_bk"][None]).reshape(HEADS_C, 96).T,
        "bo_c": cols(L1["attn_bo"]),
        "b1": L1["ffn_b1"].T,
        "ident": np.eye(128, dtype=f32),
        "centring": np.eye(128, dtype=f32) - f32(1.0 / 128),
        "mean_w": np.full((128, 1), 1.0 / 128, f32),
        "band": band,
        "eps": np.full((128, 1), LN_EPS, f32),
        "iota": np.broadcast_to(np.tile(np.arange(EXPERTS, dtype=f32), TT), (128, TT * EXPERTS)),
    }
    for name in ("bq_c", "bk_c"):
        parts[name] = np.concatenate([parts[name], np.zeros((32, HEADS_C), f32)], 0)
    for name, width in SECTIONS:
        assert parts[name].shape == (128, width), (name, parts[name].shape)
    arrays = {
        "x_dram": np.ascontiguousarray(a["x"].reshape(IMAGES, C, TOK)),
        "x_by_window_dram": np.ascontiguousarray(a["x"].reshape(IMAGES, C, WIN_SIDE, 2, WIN_SIDE, 2)
                                                 .transpose(0, 1, 3, 5, 2, 4)).reshape(IMAGES, C, TOK),
        "packed_dram": np.ascontiguousarray(np.concatenate([parts[name] for name, _ in SECTIONS], 1)),
        "gains_dram": np.ascontiguousarray(np.concatenate(
            [everywhere(np.concatenate([L0["gq"], L0["gkv"], L0["g_fc2"]])), dw, eye], 1)),
    }
    nc = bacc.Bacc("TRN2", target_bir_lowering=False, num_devices=1)
    args = [nc.dram_tensor(k, v.shape, F32, kind="ExternalInput").ap() for k, v in arrays.items()]
    out = nc.dram_tensor("out_dram", (IMAGES, TOK, C), F32, kind="ExternalOutput").ap()
    table = nc.dram_tensor("window_table", (WINS, PX * 2 * C), F32).ap()
    hybrid_layers(nc, *args, out, table)
    r = run_bass_kernel_spmd(nc, [arrays], core_ids=[0])
    got = r.results[0]["out_dram"]
    return np.ascontiguousarray(got.transpose(0, 2, 1)).reshape(IMAGES, C, SIDE, SIDE)
```
